# Optimizing a Trainium2 kernel written in Bass

```python
import numpy as np
import jax
import jax.numpy as jnp

def _softmax(x, axis=-1):
    return jax.nn.softmax(x, axis=axis)

def _gelu(x):
    return jax.nn.gelu(x, approximate=True)

def _silu(x):
    return jax.nn.silu(x)

def _sigmoid(x):
    return jax.nn.sigmoid(x)

def _layernorm(x, axis=-1, eps=1e-05):
    m = jnp.mean(x, axis=axis, keepdims=True)
    v = jnp.var(x, axis=axis, keepdims=True)
    return (x - m) / jnp.sqrt(v + eps)

def _scatter_add(tgt, idx, src, axis=0):
    return tgt.at[idx].add(src)

def _segment_sum(src, seg, n):
    return jax.ops.segment_sum(src, seg, n)
kernel_name = 'mk_adj_ffn_d1_adj_r2_215cf8'

def setup_inputs(seed: int=0):
    np.random.seed(seed)
    _w = jnp.asarray

    def _rec_inputs():
        import jax
        import jax.numpy as jnp
        _gk = jax.random.key(seed)
        x = -0.0002928 + 1 * jax.random.normal(jax.random.fold_in(_gk, 1), (64, 128, 128), jnp.float32)
        _a = jax.random.bernoulli(jax.random.fold_in(_gk, 2), 0.0625, (64, 128, 128))
        _a = jnp.logical_or(_a, jnp.swapaxes(_a, -1, -2))
        _a = jnp.logical_or(_a, jnp.eye(128, dtype=bool))
        adj = _a.astype(jnp.int32)
        return (x, adj)
    x, adj = _rec_inputs()

    def _L0_gnn_setup():
        import jax, jax.numpy as jnp
        import numpy as np
        NEG_INF = -1000000000.0
        LEAKY_SLOPE = 0.2
        key = jax.random.key(seed)
        k1, k2, k3, k4 = jax.random.split(key, 4)
        B, N, D_in, D_out = (8, 1024, 128, 128)
        x = jax.random.normal(k1, (B, N, D_in), dtype=jnp.float32)
        adj_matrix = jax.random.randint(k2, (B, N, N), 0, 2, dtype=jnp.int32)
        W = jax.random.normal(k3, (D_out, D_in), dtype=jnp.float32) / np.sqrt(D_in)
        a = jax.random.normal(k4, (1, 2 * D_out), dtype=jnp.float32) / np.sqrt(2 * D_out)
        return {'x': x, 'adj_matrix': adj_matrix, 'W': W, 'a': a}
    _L0_gnn_all = _L0_gnn_setup()
    _L0_gnn_in = {k: v for k, v in _L0_gnn_all.items() if k in ('W', 'a')}
    del _L0_gnn_all

    def _L0_ffn_setup():
        import jax, jax.numpy as jnp
        import numpy as np
        B, S, H, F, E, K = (8, 2048, 128, 256, 16, 2)
        EPS = 1e-05
        key = jax.random.key(seed)
        ks = jax.random.split(key, 9)
        sc = 0.02
        return {'x': jax.random.normal(ks[0], (B, S, H), dtype=jnp.float32), 'gate_w': jax.random.normal(ks[1], (H, E), dtype=jnp.float32) * sc, 'gate_b': jnp.zeros((E,), dtype=jnp.float32), 'w1': jax.random.normal(ks[2], (E, H, F), dtype=jnp.float32) * sc, 'b1': jnp.zeros((E, F), dtype=jnp.float32), 'w2': jax.random.normal(ks[3], (E, F, H), dtype=jnp.float32) * sc, 'b2': jnp.zeros((E, H), dtype=jnp.float32), 'gamma': jnp.ones((H,), dtype=jnp.float32), 'beta': jnp.zeros((H,), dtype=jnp.float32)}
    _L0_ffn_all = _L0_ffn_setup()
    _L0_ffn_in = {k: v for k, v in _L0_ffn_all.items() if k in ('gate_w', 'gate_b', 'w1', 'b1', 'w2', 'b2', 'gamma', 'beta')}
    del _L0_ffn_all
    return {'x': x, 'adj': adj, 'L0_gnn_W': _L0_gnn_in['W'], 'L0_gnn_a': _L0_gnn_in['a'], 'L0_ffn_gate_w': _L0_ffn_in['gate_w'], 'L0_ffn_gate_b': _L0_ffn_in['gate_b'], 'L0_ffn_w1': _L0_ffn_in['w1'], 'L0_ffn_b1': _L0_ffn_in['b1'], 'L0_ffn_w2': _L0_ffn_in['w2'], 'L0_ffn_b2': _L0_ffn_in['b2'], 'L0_ffn_gamma': _L0_ffn_in['gamma'], 'L0_ffn_beta': _L0_ffn_in['beta']}

def reference(x, adj, L0_gnn_W, L0_gnn_a, L0_ffn_gate_w, L0_ffn_gate_b, L0_ffn_w1, L0_ffn_b1, L0_ffn_w2, L0_ffn_b2, L0_ffn_gamma, L0_ffn_beta):
    import jax
    import jax.numpy as jnp

    def _L0_gnn_ref(x, adj_matrix, W, a):
        import jax, jax.numpy as jnp
        import numpy as np
        NEG_INF = -1000000000.0
        LEAKY_SLOPE = 0.2
        h = jnp.einsum('bnd,od->bno', x, W)
        D = h.shape[-1]
        a_left, a_right = (a[0, :D], a[0, D:])
        e = (h @ a_left)[:, :, None] + (h @ a_right)[:, None, :]
        e = jnp.where(e > 0, e, LEAKY_SLOPE * e)
        e = jnp.where(adj_matrix == 0, NEG_INF, e)
        alpha = jax.nn.softmax(e, axis=-1)
        return jnp.einsum('bij,bjd->bid', alpha, h)

    def _L0_ffn_ref(x, gate_w, gate_b, w1, b1, w2, b2, gamma, beta):
        import jax, jax.numpy as jnp
        import numpy as np
        B, S, H, F, E, K = (8, 2048, 128, 256, 16, 2)
        EPS = 1e-05
        gate_logits = x @ gate_w + gate_b
        topk_vals, topk_idx = jax.lax.top_k(gate_logits, K)
        topk_w = jax.nn.softmax(topk_vals, axis=-1)
        h = jax.nn.relu(jnp.einsum('bsh,ehf->bsef', x, w1) + b1)
        expert_out = jnp.einsum('bsef,efh->bseh', h, w2) + b2
        sel = jnp.take_along_axis(expert_out, topk_idx[:, :, :, None], axis=2)
        moe = jnp.sum(topk_w[..., None] * sel, axis=2)
        y = x + moe
        mu = jnp.mean(y, axis=-1, keepdims=True)
        var = jnp.var(y, axis=-1, keepdims=True)
        return (y - mu) / jnp.sqrt(var + EPS) * gamma + beta
    x = x + _L0_gnn_ref(_layernorm(x, axis=-1), adj, L0_gnn_W, L0_gnn_a)
    x = x + _L0_ffn_ref(_layernorm(x, axis=-1), L0_ffn_gate_w, L0_ffn_gate_b, L0_ffn_w1, L0_ffn_b1, L0_ffn_w2, L0_ffn_b2, L0_ffn_gamma, L0_ffn_beta)
    return x

_drawn_inputs = setup_inputs


def setup_inputs(seed=0):
    import zlib

    import numpy as np

    out = dict(_drawn_inputs(seed))
    spreads = {'L0_ffn_gate_b': (0.0, 0.1),
     'L0_ffn_b1': (0.0, 0.8),
     'L0_ffn_b2': (0.0, 0.1),
     'L0_ffn_gamma': (1.0, 0.2),
     'L0_ffn_beta': (0.0, 0.1)}
    factors = {'L0_ffn_w1': 3.696, 'L0_ffn_w2': 2.906}
    for name, (base, spread) in spreads.items():
        noise = np.random.default_rng([zlib.crc32(name.encode()), seed]).standard_normal(out[name].shape)
        drawn = base * np.exp(spread * noise) if base else spread * noise
        out[name] = jnp.asarray(drawn.astype(out[name].dtype))
    for name, factor in factors.items():
        out[name] = (out[name] * factor).astype(out[name].dtype)
    return out
```

```python
from contextlib import ExitStack

import concourse.bass as bass
from concourse import mybir

F32 = mybir.dt.float32
BF16 = mybir.dt.bfloat16
I32 = mybir.dt.int32
U32 = mybir.dt.uint32
ALU = mybir.AluOpType
ACT = mybir.ActivationFunctionType
X = mybir.AxisListType.X

P = 128
G, N, D = 64, 128, 128
E, F, K = 16, 256, 2
FH = F // P
CH = 8
NC = G // CH
GR = 4
TOK = G * N
REGION = TOK + P
PAIRS = 72
TILES = 2 * PAIRS
SPARE = TILES - TOK * K // P
SLOPE = 0.2
EPS = 1e-5
FAR = -1e30
WB = F + FH
DVE_CHUNKS = 110
assert TILES >= TOK * K // P + E - 1


class Steps:

    def __init__(self, eng, sem):
        self.eng, self.sem, self.base, self.n = eng, sem, 0, 0

    def did(self, ins):
        ins.then_inc(self.sem, 1)
        self.n += 1
        return self.n

    def wait(self, n):
        self.eng.wait_ge(self.sem, self.base + n)


def build(nc, x, adj, W, a, gate_w, gate_b, w1, b1, w2, b2, gamma, beta, out):
    xs_buf = nc.dram_tensor("expert_rows", (E * REGION + SPARE * P, D), F32, kind="Internal").ap()
    y_buf = nc.dram_tensor("expert_outs", (TILES * P, D), F32, kind="Internal").ap()
    x1_buf = nc.dram_tensor("x1_rows", (NC, P, CH * D), F32, kind="Internal").ap()
    u_buf = nc.dram_tensor("u_rows", (NC, P, CH * D), F32, kind="Internal").ap()
    x_v = x.rearrange("(c k) n d -> c n k d", k=CH)
    adj_v = adj.rearrange("(c k) n m -> c n k m", k=CH)
    out_v = out.rearrange("(c k) n d -> c n k d", k=CH)
    x1_v = x1_buf.rearrange("c n (k d) -> c n k d", k=CH)
    u_v = u_buf.rearrange("c n (k d) -> c n k d", k=CH)
    y_v = y_buf.rearrange("(k t p) d -> t p k d", k=2, p=P)

    with ExitStack() as ctx:
        def sb(name, shape, dt=F32):
            return ctx.enter_context(nc.sbuf_tensor(name, shape, dt))

        def sem(name):
            return ctx.enter_context(nc.semaphore(name))

        bank = [ctx.enter_context(nc.psum_tensor(f"bank{i}", [P, 512], F32)) for i in range(8)]
        ps_xT, ps_h, ps_pT, ps_pv, ps_uT, ps_gate = (bank[i] for i in (0, 1, 4, 5, 6, 7))
        ps_z = [bank[2], bank[3]]
        ps_hid = [bank[1], bank[2]]
        ps_y = [bank[3], bank[4]]

        ident = sb("ident", [P, P])
        ident_b = sb("ident_b", [P, P], BF16)
        ones_b = sb("ones_b", [P, P], BF16)
        before_b = sb("before_b", [P, P], BF16)
        cum48 = sb("cum48", [E, 3 * E], BF16)
        zeros = sb("zeros", [P, SPARE, D])
        W_sb = sb("W_sb", [P, D])
        a_sb = sb("a_sb", [P, 2])
        WT = sb("WT", [P, D])
        v_rep = sb("v_rep", [P, 2, P])
        gw = sb("gw", [P, E])
        gb = sb("gb", [P, E])
        w1_sb = sb("w1_sb", [P, E * WB])
        w2_sb = sb("w2_sb", [P, E * FH * D])
        b2_sb = sb("b2_sb", [P, E * D])
        gamma_sb = sb("gamma_sb", [P, D])
        beta_sb = sb("beta_sb", [P, D])
        iota_e = sb("iota_e", [P, E])
        region = sb("region", [P, E])
        iota_t = sb("iota_t", [P, 2])

        xs = [sb(f"xs{i}", [P, CH, D]) for i in range(2)]
        adj_sb = [sb(f"adj{i}", [P, CH, N], I32) for i in range(2)]
        xn = [sb(f"xn{i}", [P, CH, D]) for i in range(2)]
        x1 = [sb(f"x1{i}", [P, CH, D]) for i in range(2)]
        u = [sb(f"u{i}", [P, CH, D]) for i in range(2)]
        xT = [sb(f"xT{i}", [P, GR * N]) for i in range(2)]
        h_sb = [sb(f"h{i}", [P, GR * D]) for i in range(2)]
        mask = [sb(f"mask{i}", [P, GR * N], BF16) for i in range(2)]
        z02 = [sb(f"z02_{i}", [P, GR * N]) for i in range(2)]
        score = [sb(f"score{i}", [P, GR, N]) for i in range(2)]
        prob = [sb(f"prob{i}", [P, GR, N]) for i in range(2)]
        pT = [sb(f"pT{i}", [P, GR * N]) for i in range(2)]
        uT = [sb(f"uT{i}", [P, GR * N]) for i in range(2)]
        negmax = [sb(f"negmax{i}", [P, GR]) for i in range(2)]
        sums = [sb(f"sums{i}", [P, GR]) for i in range(2)]
        rsum = [sb(f"rsum{i}", [P, GR]) for i in range(2)]
        stat = sb("stat", [P, 2 * CH, 6])
        nrm = sb("nrm", [P, 10, 2 * CH])
        lg = sb("lg", [P, CH, E])
        l2 = sb("l2", [P, CH, E])
        eq = sb("eq", [P, CH, E])
        cand = sb("cand", [P, CH, E])
        top = sb("top", [P, 8, CH])
        oh = sb("oh", [P, K, CH, E])
        both_b = sb("both_b", [P, CH, E], BF16)
        rank = sb("rank", [P, CH, E])
        picked = sb("picked", [P, K, CH, E])
        pos = [sb(f"pos{i}", [P, K * CH], U32) for i in range(2)]
        posf = sb("posf", [P, K * CH])
        seen = sb("seen", [P, E])
        seen_new = sb("seen_new", [P, E])
        seen_b = sb("seen_b", [P, E], BF16)
        oh_all = sb("oh_all", [P, NC * K * CH, E], BF16)
        pos_all = sb("pos_all", [P, NC * K * CH])
        wt_all = sb("wt_all", [P, NC * K * CH])
        tiles_i = sb("tiles_i", [E, P], I32)
        tiles_b = sb("tiles_b", [E, P], BF16)
        cums = sb("cums", [P, 3 * E])
        tab = sb("tab", [P, 8])
        tab_cmp = sb("tab_cmp", [P, 2, E])
        tab_mul = sb("tab_mul", [P, 2, E])
        skip = sb("skip", [P, E])
        tab_i = sb("tab_i", [4, P], I32)
        tail_i = sb("tail_i", [P, E], I32)
        shift = sb("shift", [P, E])
        moved = sb("moved", [P, NC * K * CH, E])
        shifts = sb("shifts", [P, NC * K * CH])
        slot_all = sb("slot_all", [P, NC * K * CH], U32)
        rows = [sb(f"rows{i}", [P, D]) for i in range(4)]
        rowsT = [sb(f"rowsT{i}", [P, 2 * P]) for i in range(2)]
        w1t = [sb(f"w1t{i}", [P, WB]) for i in range(4)]
        hid = [sb(f"hid{i}", [P, FH * P]) for i in range(4)]
        y_sb = [sb(f"y_sb{i}", [P, 2, D]) for i in range(2)]
        got = [sb(f"got{i}", [P, K * CH, D]) for i in range(2)]
        slot = [sb(f"slot{i}", [P, K * CH], U32) for i in range(2)]
        wt = sb("wt", [P, K * CH])
        acc = sb("acc", [P, CH, D])

        def sems(names):
            return [sem(n) for n in names.split()]

        (pool_turns, small_in, loaded, ones_set, ident_set, consts, vec_done, pool_done, prep_done, prep_copied) = sems(
            "pool_turns small_in loaded ones_set ident_set consts vec_done pool_done prep_done prep_copied")
        x_in = [sem("x_in0"), sem("x_in1")]
        adj_in = [sem("adj_in0"), sem("adj_in1")]
        (xn_ready, xT_done, xT_ready, h_done, h_ready, mask_ready, z_done, y_ready, max_ready,
         exp_ready, pT_done, pT_ready, pv_done, x1_done, var_ready, sd_ready, u_ready, uT_done,
         uT_ready, gate_done, both_ready, rank_done, gap_ready, odds_ready, pos_ready) = sems(
            "xn_ready xT_done xT_ready h_done h_ready mask_ready z_done y_ready max_ready "
            "exp_ready pT_done pT_ready pv_done x1_done var_ready sd_ready u_ready uT_done "
            "uT_ready gate_done both_ready rank_done gap_ready odds_ready pos_ready")
        x1_out = [sem("x1_out0"), sem("x1_out1")]
        u_out = [sem("u_out0"), sem("u_out1")]
        sent = [sem("sent0"), sem("sent1")]
        zeroed, seen_ready, count_done, tiles_ready, cum_done, tab_ready, tab_done, tables_ready, tails_ready = sems(
            "zeroed seen_ready count_done tiles_ready cum_done tab_ready tab_done tables_ready tails_ready")
        rows_in = [sem(f"rows_in{i}") for i in range(4)]
        rowsT_done, rowsT_ready, w1_ready, hid_done, hid_ready, y_done, y_added = sems(
            "rowsT_done rowsT_ready w1_ready hid_done hid_ready y_done y_added")
        y_out = [sem("y_out0"), sem("y_out1")]
        slot_ready, c_var, c_sd, out_ready = sems("slot_ready c_var c_sd out_ready")
        fetched = [sem("fetched0"), sem("fetched1")]
        c_in = [sem("c_in0"), sem("c_in1")]
        out_done = [sem("out_done0"), sem("out_done1")]

        SMALL = 4
        LOADS = 7
        POOL_CONSTS = 10
        block = ctx.enter_context(nc.Block())

        @block.sync
        def _(sp):
            def load_chunk(c, par):
                sp.dma_start(xs[par][:], x_v[c]).then_inc(x_in[par], 16)
                sp.dma_start(adj_sb[par][:], adj_v[c]).then_inc(adj_in[par], 16)

            sp.dma_start(xs[0][:], x_v[0]).then_inc(x_in[0], 16)
            with nc.allow_non_contiguous_dma(reason="vectors with one element to a partition"):
                sp.dma_start(W_sb[:], W).then_inc(small_in, 16)
                sp.dma_start(a_sb[:], a.rearrange("r (k o) -> o (r k)", k=2)).then_inc(small_in, 16)
                sp.dma_start(adj_sb[0][:], adj_v[0]).then_inc(adj_in[0], 16)
                sp.dma_start(gw[:], gate_w).then_inc(small_in, 16)
                sp.dma_start(gb[:], gate_b.rearrange("(o e) -> o e", o=1).to_broadcast([P, E])).then_inc(small_in, 16)
                load_chunk(1, 1)
                w1_v = w1_sb[:].rearrange("p (e f) -> p e f", e=E)
                sp.dma_start(w1_v[:, :, 0:F], w1.rearrange("e h f -> h e f")).then_inc(loaded, 16)
                for j in range(FH):
                    sp.dma_start(w1_v[:, :, F + j], b1[:, j * P:(j + 1) * P].rearrange("e p -> p e")).then_inc(loaded, 16)
                sp.dma_start(w2_sb[:].rearrange("p (e j d) -> p e j d", e=E, j=FH),
                             w2.rearrange("e (j p) d -> p e j d", p=P)).then_inc(loaded, 16)
                sp.dma_start(b2_sb[:], b2.rearrange("(o e) d -> o (e d)", o=1).to_broadcast([P, E * D])).then_inc(loaded, 16)
                sp.dma_start(gamma_sb[:], gamma.rearrange("(o d) -> o d", o=1).to_broadcast([P, D])).then_inc(loaded, 16)
                sp.dma_start(beta_sb[:], beta.rearrange("(o d) -> o d", o=1).to_broadcast([P, D])).then_inc(loaded, 16)
            sp.wait_ge(ones_set, 1)
            sp.dma_start(xs_buf[E * REGION:, :].rearrange("(t p) d -> p t d", p=P), zeros[:]).then_inc(zeroed, 16)

            def attention_io(it, par, ahead):
                c = 2 * it + par
                sp.wait_ge(x1_done, 2 * c + 2)
                sp.dma_start(x1_v[c], x1[par][:]).then_inc(x1_out[par], 16)
                if ahead:
                    load_chunk(c + 2, par)
                sp.wait_ge(u_ready, 2 * c + 2)
                sp.dma_start(u_v[c], u[par][:]).then_inc(u_out[par], 16)

            with sp.Fori(0, NC // 2 - 1) as it:
                for par in range(2):
                    attention_io(it, par, True)
            for par in range(2):
                attention_io(NC // 2 - 1, par, False)

            sp.wait_ge(tails_ready, 1)
            with sp.Fori(0, E) as e:
                start = sp.value_load(tail_i[0:1, bass.ds(e, 1)], min_val=0, max_val=E * REGION - P)
                sp.dma_start(xs_buf[bass.ds(start, P), :], zeros[:, 0, :]).then_inc(zeroed, 16)
            sp.wait_ge(tables_ready, 1)
            sp.wait_ge(zeroed, 16 * (E + 1))
            for par in range(2):
                sp.wait_ge(sent[par], NC // 2 * CH * K * 16)

            def load_rows(i, q, half):
                for k in range(2):
                    row = sp.value_load(tab_i[2 + k:3 + k, bass.ds(i, 1)], min_val=0,
                                        max_val=E * REGION + (SPARE - 1) * P)
                    sp.dma_start(rows[2 * q + k][:], xs_buf[bass.ds(row, P), :]).then_inc(rows_in[2 * q + k], 16)

            def store_y(i, q):
                sp.wait_ge(y_added, i + 1)
                sp.dma_start(y_v[i], y_sb[q][:]).then_inc(y_out[q], 16)

            for q in range(2):
                load_rows(q, q, 0)
            with sp.Fori(0, PAIRS // 2 - 1) as half:
                for q in range(2):
                    i = 2 * half + q
                    sp.wait_ge(rowsT_done, i + 1)
                    load_rows(i + 2, q, half + 1)
                    store_y(i, q)
            for q in range(2):
                store_y(PAIRS - 2 + q, q)

            def load_tokens(c, par):
                sp.dma_start(x1[par][:], x1_v[c]).then_inc(c_in[par], 16)
                sp.dma_start(u[par][:], u_v[c]).then_inc(c_in[par], 16)

            for par in range(2):
                sp.wait_ge(x1_out[par], 16 * (NC // 2))
                sp.wait_ge(u_out[par], 16 * (NC // 2))
                load_tokens(par, par)

            def combine_io(it, par, ahead):
                c = 2 * it + par
                sp.wait_ge(out_ready, c + 1)
                sp.dma_start(out_v[c], xn[par][:]).then_inc(out_done[par], 16)
                if ahead:
                    load_tokens(c + 2, par)

            with sp.Fori(0, NC // 2 - 1) as it:
                for par in range(2):
                    combine_io(it, par, True)
            for par in range(2):
                combine_io(NC // 2 - 1, par, False)
            for par in range(2):
                sp.wait_ge(out_done[par], 16 * (NC // 2))

        @block.vector
        def _(dve):
            v = nc.vector
            S = Steps(dve, vec_done)

            def bc(ap, shape):
                return ap.to_broadcast(shape)

            def mean_and_var(n0, n1):
                w = slice(n0, n1)
                me, qe, mo, qo = (stat[:, w, i] for i in (1, 2, 4, 5))
                s = [S.did(v.tensor_tensor(nrm[:, 1, w], me, mo, ALU.add)),
                     S.did(v.tensor_tensor(nrm[:, 2, w], me, mo, ALU.subtract)),
                     S.did(v.tensor_tensor(nrm[:, 3, w], qe, qo, ALU.add))]
                S.wait(s[0])
                S.did(v.tensor_scalar(nrm[:, 0, w], nrm[:, 1, w], 0.5, None, ALU.mult))
                S.wait(s[1])
                t = S.did(v.scalar_tensor_tensor(out=nrm[:, 4, w], in0=nrm[:, 2, w], scalar=0.25,
                                                 in1=nrm[:, 2, w], op0=ALU.mult, op1=ALU.mult))
                S.wait(s[2])
                t = S.did(v.tensor_scalar(nrm[:, 5, w], nrm[:, 3, w], 1.0 / D, EPS, ALU.mult, ALU.add))
                S.wait(t)
                return v.tensor_tensor(nrm[:, 6, w], nrm[:, 4, w], nrm[:, 5, w], ALU.add)

            def rstd(n0, n1):
                w = slice(n0, n1)
                S.wait(S.did(v.reciprocal(nrm[:, 8, w], nrm[:, 7, w])))
                S.wait(S.did(v.tensor_tensor(nrm[:, 1, w], nrm[:, 8, w], nrm[:, 8, w], ALU.mult)))
                S.wait(S.did(v.tensor_tensor(nrm[:, 2, w], nrm[:, 1, w], nrm[:, 6, w], ALU.mult)))
                S.wait(S.did(v.tensor_scalar(nrm[:, 3, w], nrm[:, 2, w], -0.5, 1.5, ALU.mult, ALU.add)))
                S.wait(S.did(v.tensor_tensor(nrm[:, 9, w], nrm[:, 3, w], nrm[:, 8, w], ALU.mult)))

            def normed(dst, src, col):
                return v.tensor_scalar(dst, src, nrm[:, 0, col:col + 1], nrm[:, 9, col:col + 1],
                                       ALU.subtract, ALU.mult)

            v.memset(zeros[:], 0.0).then_inc(ones_set, 1)
            v.memset(ones_b[:], 1.0).then_inc(ones_set, 1)
            S.did(v.memset(seen[:], 0.0))
            s0 = S.did(v.memset(seen_b[:], 0.0))
            dve.wait_ge(ident_set, 1)
            v.tensor_copy(ident_b[:], ident[:]).then_inc(consts, 1)
            dve.wait_ge(x_in[0], 16)
            for k in range(CH):
                s = S.did(v.bn_stats(stat[:, CH + k, :], xs[0][:, k, :]))
            S.wait(s)
            mean_and_var(CH, 2 * CH).then_inc(var_ready, 1)
            dve.wait_ge(prep_done, 1)
            v.tensor_copy(WT[:], ps_h[:, 0:D]).then_inc(prep_copied, 1)
            dve.wait_ge(prep_done, 2)
            v.tensor_copy(v_rep[:], bc(ps_h[:, 0:2].unsqueeze(2), [P, 2, P])).then_inc(prep_copied, 1)
            dve.wait_ge(sd_ready, 1)
            rstd(CH, 2 * CH)
            for k in range(CH):
                ins = normed(xn[0][:, k, :], xs[0][:, k, :], CH + k)
                if k % GR == GR - 1:
                    ins.then_inc(xn_ready, 1)
            dve.wait_ge(small_in, 16 * SMALL)
            dve.wait_ge(pool_done, POOL_CONSTS)
            prologue = S.n

            def chunk(it, par, last):
                c = 2 * it + par
                for g in range(2):
                    if g == 0:
                        dve.wait_ge(adj_in[par], 16 * (it + 1))
                    v.tensor_scalar(mask[g][:], adj_sb[par][:, g * GR:(g + 1) * GR, :].rearrange("p k n -> p (k n)"),
                                    0.0, FAR, ALU.is_equal, ALU.mult).then_inc(mask_ready, 1)
                for g in range(2):
                    dve.wait_ge(y_ready, 2 * c + g + 1)
                    s = S.did(v.tensor_tensor(score[g][:].rearrange("p k n -> p (k n)"), ps_z[g][:], z02[g][:], ALU.max))
                    S.wait(s)
                    v.tensor_reduce(negmax[g][:], score[g][:], X, ALU.max, negate=True).then_inc(max_ready, 1)
                if not last:
                    dve.wait_ge(x_in[1 - par], 16 * (it + 1 + par))
                    for k in range(CH):
                        S.did(v.bn_stats(stat[:, CH + k, :], xs[1 - par][:, k, :]))
                dve.wait_ge(x1_out[par], 16 * it)
                for g in range(2):
                    dve.wait_ge(pv_done, 2 * c + g + 1)
                    S.wait(S.did(v.reciprocal(rsum[g][:], sums[g][:])))
                    for k in range(GR):
                        ins = v.scalar_tensor_tensor(out=x1[par][:, g * GR + k, :], in0=ps_pv[:, k * D:(k + 1) * D],
                                                     scalar=rsum[g][:, k:k + 1], in1=xs[par][:, g * GR + k, :],
                                                     op0=ALU.mult, op1=ALU.add)
                    ins.then_inc(x1_done, 1)
                    dve.wait_ge(x1_done, 2 * c + g + 1)
                    for k in range(GR):
                        s = S.did(v.bn_stats(stat[:, g * GR + k, :], x1[par][:, g * GR + k, :]))
                S.wait(s)
                mean_and_var(0, 2 * CH).then_inc(var_ready, 1)
                dve.wait_ge(sd_ready, c + 2)
                rstd(0, 2 * CH)
                dve.wait_ge(sent[par], CH * K * 16 * it)
                dve.wait_ge(u_out[par], 16 * it)
                for k in range(CH):
                    ins = normed(u[par][:, k, :], x1[par][:, k, :], k)
                    if k % GR == GR - 1:
                        ins.then_inc(u_ready, 1)
                if not last:
                    for k in range(CH):
                        ins = normed(xn[1 - par][:, k, :], xs[1 - par][:, k, :], CH + k)
                        if k % GR == GR - 1:
                            ins.then_inc(xn_ready, 1)
                gate(it, par)

            def pick(src, at, dst):
                S.wait(S.did(v.tensor_reduce(top[:, at, :], src[:], X, ALU.max)))
                S.wait(S.did(v.tensor_tensor(eq[:], src[:], bc(top[:, at, :].unsqueeze(2), [P, CH, E]), ALU.is_equal)))
                S.wait(S.did(v.scalar_tensor_tensor(out=cand[:], in0=eq[:], scalar=-64.0,
                                                    in1=bc(iota_e[:].unsqueeze(1), [P, CH, E]), op0=ALU.mult, op1=ALU.add)))
                S.wait(S.did(v.tensor_reduce(top[:, at + 1, :], cand[:], X, ALU.min)))
                S.wait(S.did(v.tensor_tensor(dst, cand[:], bc(top[:, at + 1, :].unsqueeze(2), [P, CH, E]), ALU.is_equal)))

            def gate(it, par):
                c = 2 * it + par
                dve.wait_ge(gate_done, c + 1)
                S.wait(S.did(v.tensor_tensor(lg[:], ps_gate[:, 0:CH * E].rearrange("p (k e) -> p k e", e=E),
                                             bc(gb[:].unsqueeze(1), [P, CH, E]), ALU.add)))
                pick(lg, 0, oh[:, 0])
                S.wait(S.did(v.scalar_tensor_tensor(out=l2[:], in0=oh[:, 0], scalar=FAR, in1=lg[:],
                                                    op0=ALU.mult, op1=ALU.add)))
                pick(l2, 2, oh[:, 1])
                v.tensor_tensor(both_b[:], oh[:, 0], oh[:, 1], ALU.add).then_inc(both_ready, 1)
                v.tensor_tensor(top[:, 4, :], top[:, 2, :], top[:, 0, :], ALU.subtract).then_inc(gap_ready, 1)
                S.did(v.tensor_copy(oh_all[:, bass.ds(c * (K * CH), K * CH), :],
                                    oh[:].rearrange("p j k e -> p (j k) e")))
                dve.wait_ge(odds_ready, c + 1)
                S.wait(S.did(v.tensor_scalar(top[:, 6, :], top[:, 5, :], 1.0, None, ALU.add)))
                S.wait(S.did(v.reciprocal(top[:, 7, :], top[:, 6, :])))
                S.did(v.tensor_copy(wt_all[:, bass.ds(c * (K * CH), CH)], top[:, 7, :]))
                S.did(v.tensor_tensor(wt_all[:, bass.ds(c * (K * CH) + CH, CH)], top[:, 7, :], top[:, 5, :], ALU.mult))
                dve.wait_ge(rank_done, c + 1)
                S.wait(S.did(v.tensor_tensor(rank[:], ps_gate[:, CH * E:2 * CH * E].rearrange("p (k e) -> p k e", e=E),
                                             bc(region[:].unsqueeze(1), [P, CH, E]), ALU.add)))
                for j in range(K):
                    s = S.did(v.tensor_tensor(picked[:, j], oh[:, j], rank[:], ALU.mult))
                S.wait(s)
                s = S.did(v.tensor_reduce(posf[:], picked[:].rearrange("p j k e -> p (j k) e"), X, ALU.add))
                S.wait(s)
                v.tensor_copy(pos[par][:], posf[:]).then_inc(pos_ready, 1)
                S.did(v.tensor_copy(pos_all[:, bass.ds(c * (K * CH), K * CH)], posf[:]))
                S.wait(S.did(v.tensor_reduce(seen_new[:], both_b[:].rearrange("p k e -> p e k"), X, ALU.add)))
                S.wait(S.did(v.tensor_tensor(seen[:], seen[:], seen_new[:], ALU.add)))
                v.tensor_copy(seen_b[:], seen[:]).then_inc(seen_ready, 1)

            with dve.Fori(0, NC // 2 - 1) as it:
                S.base, S.n = prologue + it * DVE_CHUNKS, 0
                for par in range(2):
                    chunk(it, par, False)
                assert S.n == DVE_CHUNKS, S.n
            S.base, S.n = prologue + (NC // 2 - 1) * DVE_CHUNKS, 0
            for par in range(2):
                chunk(NC // 2 - 1, par, par == 1)

            dve.wait_ge(loaded, 16 * LOADS)
            dve.wait_ge(count_done, 1)
            v.tensor_tensor(tail_i[:], ps_gate[:, 0:E], region[:], ALU.add).then_inc(tails_ready, 1)
            S.wait(S.did(v.tensor_scalar(tiles_i[:], ps_h[0:E, 0:P], 1.0 / P, (P - 1) / (2.0 * P), ALU.mult, ALU.add)))
            v.tensor_copy(tiles_b[:], tiles_i[:]).then_inc(tiles_ready, 1)
            dve.wait_ge(cum_done, 1)
            S.wait(S.did(v.tensor_copy(cums[:], ps_h[:, 0:3 * E])))
            s1 = S.did(v.tensor_scalar(skip[:], cums[:, 2 * E:], -1.0, float(REGION // P), ALU.mult, ALU.add))
            s = S.did(v.tensor_tensor(tab_cmp[:], bc(iota_t[:].unsqueeze(2), [P, 2, E]),
                                      bc(cums[:, 0:E].unsqueeze(1), [P, 2, E]), ALU.is_ge))
            S.wait(s)
            S.did(v.tensor_tensor(tab_mul[:], tab_cmp[:], bc(skip[:].unsqueeze(1), [P, 2, E]), ALU.mult))
            S.wait(S.did(v.tensor_reduce(tab[:, 4:6], tab_cmp[:], X, ALU.add)))
            S.did(v.tensor_scalar(tab[:, 0:2], tab[:, 4:6], float(E - 1), None, ALU.min))
            S.wait(S.did(v.tensor_reduce(tab[:, 6:8], tab_mul[:], X, ALU.add)))
            s = S.did(v.tensor_tensor(tab[:, 4:6], tab[:, 6:8], iota_t[:], ALU.add))
            S.wait(s)
            v.tensor_scalar(tab[:, 2:4], tab[:, 4:6], float(P), None, ALU.mult).then_inc(tab_ready, 1)
            dve.wait_ge(tab_done, 1)
            v.tensor_copy(tab_i[:], ps_h[0:4, 0:P]).then_inc(tables_ready, 1)

            def expert_of(i, k):
                return dve.value_load(tab_i[k:k + 1, bass.ds(i, 1)], min_val=0, max_val=E - 1)

            def expert_weights(i, q, used):
                es = [expert_of(i, k) for k in range(2)]
                if used is not None:
                    dve.wait_ge(hid_ready, used)
                for k in range(2):
                    v.tensor_scalar(w1t[2 * q + k][:], w1_sb[:, bass.ds(es[k] * WB, WB)], 1.0, None,
                                    ALU.mult).then_inc(w1_ready, 1)

            def add_bias(i, q, half):
                es = [expert_of(i, k) for k in range(2)]
                dve.wait_ge(y_out[q], 16 * half)
                for k in range(2):
                    dve.wait_ge(y_done, 2 * i + k + 1)
                    ins = v.tensor_tensor(y_sb[q][:, k, :], ps_y[k][:, 0:D], b2_sb[:, bass.ds(es[k] * D, D)], ALU.add)
                ins.then_inc(y_added, 1)

            dve.wait_ge(tables_ready, 1)
            expert_weights(0, 0, None)
            S.wait(S.did(v.scalar_tensor_tensor(out=shift[:], in0=cums[:, E:2 * E], scalar=float(P), in1=region[:],
                                                op0=ALU.mult, op1=ALU.subtract)))
            S.wait(S.did(v.tensor_tensor(moved[:], oh_all[:], bc(shift[:].unsqueeze(1), [P, NC * K * CH, E]), ALU.mult)))
            S.wait(S.did(v.tensor_reduce(shifts[:], moved[:], X, ALU.add)))
            s = S.did(v.tensor_tensor(slot_all[:], shifts[:], pos_all[:], ALU.add))
            S.wait(s)

            def expert_pair(i, q, half, last):
                if not last:
                    expert_weights(i + 1, 1 - q, 2 * i)
                add_bias(i, q, half)

            with dve.Fori(0, PAIRS // 2 - 1) as half:
                for q in range(2):
                    expert_pair(2 * half + q, q, half, False)
            for q in range(2):
                expert_pair(PAIRS - 2 + q, q, PAIRS // 2 - 1, q == 1)

            tail = S.n
            tail_base = S.base

            def slots(it, par):
                c = 2 * it + par
                v.tensor_copy(slot[par][:], slot_all[:, bass.ds(c * (K * CH), K * CH)]).then_inc(slot_ready, 1)

            def combine(it, par, ahead):
                c = 2 * it + par
                s = S.did(v.tensor_copy(wt[:], wt_all[:, bass.ds(c * (K * CH), K * CH)]))
                S.wait(s)
                dve.wait_ge(c_in[par], 32 * (it + 1))
                dve.wait_ge(fetched[par], CH * K * 16 * (it + 1))
                for j in range(K):
                    for k in range(CH):
                        s = S.did(v.scalar_tensor_tensor(out=acc[:, k, :], in0=got[par][:, j * CH + k, :],
                                                         scalar=wt[:, j * CH + k:j * CH + k + 1],
                                                         in1=u[par][:, k, :] if j == 0 else acc[:, k, :],
                                                         op0=ALU.mult, op1=ALU.add))
                        if j == 1:
                            pass
                        elif k == CH - 1:
                            S.wait(s)
                S.wait(s)
                if ahead:
                    slots(it + 1, par)
                for k in range(CH):
                    s = S.did(v.bn_stats(stat[:, k, :], acc[:, k, :]))
                S.wait(s)
                mean_and_var(0, CH).then_inc(c_var, 1)
                s = S.did(v.tensor_tensor(u[par][:], x1[par][:], bc(beta_sb[:].unsqueeze(1), [P, CH, D]), ALU.add))
                dve.wait_ge(c_sd, c + 1)
                rstd(0, CH)
                for k in range(CH):
                    s = S.did(v.scalar_tensor_tensor(out=x1[par][:, k, :], in0=acc[:, k, :], scalar=nrm[:, 0, k:k + 1],
                                                     in1=gamma_sb[:], op0=ALU.subtract, op1=ALU.mult))
                S.wait(s)
                dve.wait_ge(out_done[par], 16 * it)
                for k in range(CH):
                    ins = v.scalar_tensor_tensor(out=xn[par][:, k, :], in0=x1[par][:, k, :], scalar=nrm[:, 9, k:k + 1],
                                                 in1=u[par][:, k, :], op0=ALU.mult, op1=ALU.add)
                ins.then_inc(out_ready, 1)
                dve.wait_ge(out_ready, c + 1)

            for par in range(2):
                slots(0, par)
            per = 2 * (1 + K * CH + CH + 6 + 1 + 5 + CH)
            with dve.Fori(0, NC // 2 - 1) as it:
                S.base, S.n = tail_base + tail + it * per, 0
                for par in range(2):
                    combine(it, par, True)
                assert S.n == per, (S.n, per)
            S.base, S.n = tail_base + tail + (NC // 2 - 1) * per, 0
            for par in range(2):
                combine(NC // 2 - 1, par, False)

        @block.scalar
        def _(act):
            s = nc.scalar
            act.wait_ge(var_ready, 1)
            s.activation(nrm[:, 7, CH:], nrm[:, 6, CH:], ACT.Sqrt).then_inc(sd_ready, 1)

            def chunk(it, par):
                c = 2 * it + par
                for g in range(2):
                    act.wait_ge(xT_done, 2 * c + g + 1)
                    s.activation(xT[g][:], ps_xT[:], ACT.Copy).then_inc(xT_ready, 1)
                for g in range(2):
                    act.wait_ge(h_done, 2 * c + g + 1)
                    s.activation(h_sb[g][:], ps_h[:], ACT.Copy).then_inc(h_ready, 1)
                    act.wait_ge(z_done, 2 * c + g + 1)
                    s.activation(z02[g][:], ps_z[g][:], ACT.Copy, scale=SLOPE).then_inc(y_ready, 1)
                for g in range(2):
                    act.wait_ge(max_ready, 2 * c + g + 1)
                    for k in range(GR):
                        ins = s.activation(prob[g][:, k, :], score[g][:, k, :], ACT.Exp, bias=negmax[g][:, k:k + 1],
                                           accum_out=sums[g][:, k:k + 1])
                    ins.then_inc(exp_ready, 1)
                for g in range(2):
                    act.wait_ge(pT_done, 2 * c + g + 1)
                    s.activation(pT[g][:], ps_pT[:], ACT.Copy).then_inc(pT_ready, 1)
                act.wait_ge(var_ready, c + 2)
                s.activation(nrm[:, 7, :], nrm[:, 6, :], ACT.Sqrt).then_inc(sd_ready, 1)
                for g in range(2):
                    act.wait_ge(uT_done, 2 * c + g + 1)
                    s.activation(uT[g][:], ps_uT[:], ACT.Copy).then_inc(uT_ready, 1)
                act.wait_ge(gap_ready, c + 1)
                s.activation(top[:, 5, :], top[:, 4, :], ACT.Exp).then_inc(odds_ready, 1)

            with act.Fori(0, NC // 2) as it:
                for par in range(2):
                    chunk(it, par)

            def evacuate(i, q):
                act.wait_ge(rowsT_done, i + 1)
                s.activation(rowsT[q][:], ps_xT[:, 0:2 * P], ACT.Copy).then_inc(rowsT_ready, 1)

            def pair(i, q, last):
                for k in range(2):
                    act.wait_ge(hid_done, 2 * i + k + 1)
                    for j in range(FH):
                        ins = s.activation(hid[2 * q + k][:, j * P:(j + 1) * P], ps_hid[k][:, j * P:(j + 1) * P],
                                           ACT.Relu, bias=w1t[2 * q + k][:, F + j:F + j + 1])
                    ins.then_inc(hid_ready, 1)
                if not last:
                    evacuate(i + 1, 1 - q)

            evacuate(0, 0)
            with act.Fori(0, PAIRS // 2 - 1) as half:
                for q in range(2):
                    pair(2 * half + q, q, False)
            for q in range(2):
                pair(PAIRS - 2 + q, q, q == 1)

            with act.Fori(0, NC) as c:
                act.wait_ge(c_var, c + 1)
                s.activation(nrm[:, 7, 0:CH], nrm[:, 6, 0:CH], ACT.Sqrt).then_inc(c_sd, 1)

        @block.tensor
        def _(pe):
            t = nc.tensor

            def mm(out_, lhsT, rhs, start=True, stop=True):
                return t.matmul(out_, lhsT, rhs, start=start, stop=stop)

            pe.wait_ge(ident_set, 1)
            pe.wait_ge(small_in, 16 * SMALL)
            t.transpose(ps_h[:, 0:D], W_sb[:], ident[:]).then_inc(prep_done, 1)
            pe.wait_ge(prep_copied, 1)
            mm(ps_h[:, 0:2], W_sb[:], a_sb[:]).then_inc(prep_done, 1)
            pe.wait_ge(prep_copied, 2)
            pe.wait_ge(consts, 1)
            pe.wait_ge(pool_done, POOL_CONSTS)

            def chunk(it, par):
                c = 2 * it + par
                for g in range(2):
                    n = 2 * c + g
                    pe.wait_ge(xn_ready, n + 1)
                    pe.wait_ge(xT_ready, n)
                    for k in range(GR):
                        ins = t.transpose(ps_xT[:, k * N:(k + 1) * N], xn[par][:, g * GR + k, :], ident[:])
                    ins.then_inc(xT_done, 1)
                for g in range(2):
                    n = 2 * c + g
                    pe.wait_ge(xT_ready, n + 1)
                    pe.wait_ge(h_ready, n)
                    for k in range(GR):
                        ins = mm(ps_h[:, k * D:(k + 1) * D], xT[g][:, k * N:(k + 1) * N], WT[:])
                    ins.then_inc(h_done, 1)
                    pe.wait_ge(mask_ready, n + 1)
                    mm(ps_z[g][:], v_rep[:, 1, :], xT[g][:], True, False)
                    for k in range(GR):
                        mm(ps_z[g][:, k * N:(k + 1) * N], xT[g][:, k * N:(k + 1) * N], v_rep[:, 0, :], False, False)
                    mm(ps_z[g][:], ident_b[:], mask[g][:], False, True).then_inc(z_done, 1)
                for g in range(2):
                    n = 2 * c + g
                    pe.wait_ge(exp_ready, n + 1)
                    pe.wait_ge(pT_ready, n)
                    for k in range(GR):
                        ins = t.transpose(ps_pT[:, k * N:(k + 1) * N], prob[g][:, k, :], ident[:])
                    ins.then_inc(pT_done, 1)
                for g in range(2):
                    n = 2 * c + g
                    pe.wait_ge(pT_ready, n + 1)
                    pe.wait_ge(x1_done, n)
                    for k in range(GR):
                        ins = mm(ps_pv[:, k * D:(k + 1) * D], pT[g][:, k * N:(k + 1) * N], h_sb[g][:, k * D:(k + 1) * D])
                    ins.then_inc(pv_done, 1)
                for g in range(2):
                    n = 2 * c + g
                    pe.wait_ge(u_ready, n + 1)
                    pe.wait_ge(uT_ready, n)
                    for k in range(GR):
                        ins = t.transpose(ps_uT[:, k * N:(k + 1) * N], u[par][:, g * GR + k, :], ident[:])
                    ins.then_inc(uT_done, 1)
                pe.wait_ge(pos_ready, c)
                for g in range(2):
                    pe.wait_ge(uT_ready, 2 * c + g + 1)
                    for k in range(GR):
                        at = (g * GR + k) * E
                        ins = mm(ps_gate[:, at:at + E], uT[g][:, k * N:(k + 1) * N], gw[:])
                ins.then_inc(gate_done, 1)
                pe.wait_ge(both_ready, c + 1)
                flat = both_b[:].rearrange("p k e -> p (k e)")
                w = CH * E
                mm(ps_gate[:, w:2 * w], before_b[:], flat, True, False)
                for k in range(1, CH):
                    mm(ps_gate[:, w + k * E:2 * w], ones_b[:], flat[:, 0:(CH - k) * E], False, False)
                pe.wait_ge(seen_ready, c)
                mm(ps_gate[:, w:2 * w], ones_b[:], seen_b[:].unsqueeze(1).to_broadcast([P, CH, E]),
                   False, True).then_inc(rank_done, 1)

            with pe.Fori(0, NC // 2) as it:
                for par in range(2):
                    chunk(it, par)

            pe.wait_ge(seen_ready, NC)
            mm(ps_gate[:, 0:E], ones_b[:], seen_b[:])
            mm(ps_h[0:E, 0:P], seen_b[:], ones_b[:]).then_inc(count_done, 1)
            pe.wait_ge(tiles_ready, 1)
            mm(ps_h[:, 0:3 * E], tiles_b[:], cum48[:]).then_inc(cum_done, 1)
            pe.wait_ge(tab_ready, 1)
            t.transpose(ps_h[0:4, 0:P], tab[:, 0:4], ident[:]).then_inc(tab_done, 1)
            pe.wait_ge(tables_ready, 1)

            def turn(i, q, half):
                for k in range(2):
                    pe.wait_ge(rows_in[2 * q + k], 16 * (half + 1))
                pe.wait_ge(rowsT_ready, i)
                for k in range(2):
                    ins = t.transpose(ps_xT[:, k * P:(k + 1) * P], rows[2 * q + k][:], ident[:])
                ins.then_inc(rowsT_done, 1)

            def pair(i, q, half, last):
                pe.wait_ge(rowsT_ready, i + 1)
                pe.wait_ge(w1_ready, 2 * i + 2)
                for k in range(2):
                    pe.wait_ge(hid_ready, 2 * i)
                    for j in range(FH):
                        ins = mm(ps_hid[k][:, j * P:(j + 1) * P], w1t[2 * q + k][:, j * P:(j + 1) * P],
                                 rowsT[q][:, k * P:(k + 1) * P])
                    ins.then_inc(hid_done, 1)
                if not last:
                    turn(i + 1, 1 - q, half + q)
                pe.wait_ge(y_added, i)
                for k in range(2):
                    e = pe.value_load(tab_i[k:k + 1, bass.ds(i, 1)], min_val=0, max_val=E - 1)
                    pe.wait_ge(hid_ready, 2 * i + k + 1)
                    for j in range(FH):
                        ins = mm(ps_y[k][:, 0:D], hid[2 * q + k][:, j * P:(j + 1) * P],
                                 w2_sb[:, bass.ds(e * (FH * D) + j * D, D)], j == 0, j == FH - 1)
                    ins.then_inc(y_done, 1)

            turn(0, 0, 0)
            with pe.Fori(0, PAIRS // 2 - 1) as half:
                for q in range(2):
                    pair(2 * half + q, q, half, False)
            for q in range(2):
                pair(PAIRS - 2 + q, q, PAIRS // 2 - 1, q == 1)

        @block.gpsimd
        def _(pool):
            p = nc.gpsimd
            S = Steps(pool, pool_done)
            S.wait(S.did(p.memset(ident[:], 1.0)))
            p.affine_select(ident[:], ident[:], pattern=[[-1, P]], compare_op=ALU.is_equal, fill=0.0, base=0,
                            channel_multiplier=1).then_inc(ident_set, 1)
            S.did(p.memset(cum48[:], 1.0))
            S.wait(S.did(p.memset(before_b[:], 1.0)))
            S.did(p.affine_select(before_b[:], before_b[:], pattern=[[1, P]], compare_op=ALU.is_gt, fill=0.0, base=0,
                                  channel_multiplier=-1))
            for n, op in enumerate((ALU.is_ge, ALU.is_gt, ALU.is_equal)):
                S.did(p.affine_select(cum48[:, n * E:(n + 1) * E], cum48[:, n * E:(n + 1) * E], pattern=[[1, E]],
                                      compare_op=op, fill=0.0, base=0, channel_multiplier=-1))
            S.did(p.iota(iota_e[:], pattern=[[1, E]], base=0, channel_multiplier=0, allow_small_or_imprecise_dtypes=True))
            S.did(p.iota(region[:], pattern=[[REGION, E]], base=0, channel_multiplier=0, allow_small_or_imprecise_dtypes=True))
            p.iota(iota_t[:], pattern=[[PAIRS, 2]], base=0, channel_multiplier=1,
                   allow_small_or_imprecise_dtypes=True).then_inc(pool_done, 1)

            with pool.Fori(0, NC // 2) as it:
                for par in range(2):
                    pool.wait_ge(pos_ready, 2 * it + par + 1)
                    pool.sem_inc(pool_turns, 1)
                    for j in range(K):
                        for k in range(CH):
                            p.indirect_dma_start(xs_buf, bass.IndirectOffsetOnAxis(ap=pos[par][:, j * CH + k:j * CH + k + 1], axis=0),
                                                 u[par][:, k, :], None).then_inc(sent[par], 16)

            for q in range(2):
                pool.wait_ge(y_out[q], 16 * (PAIRS // 2))
            with pool.Fori(0, NC // 2) as it:
                for par in range(2):
                    pool.wait_ge(slot_ready, 2 * it + par + 1)
                    pool.sem_inc(pool_turns, 1)
                    for j in range(K):
                        for k in range(CH):
                            at = j * CH + k
                            p.indirect_dma_start(got[par][:, at, :], None, y_buf,
                                                 bass.IndirectOffsetOnAxis(ap=slot[par][:, at:at + 1], axis=0)).then_inc(fetched[par], 16)


_INS = ["x", "adj", "L0_gnn_W", "L0_gnn_a", "L0_ffn_gate_w", "L0_ffn_gate_b", "L0_ffn_w1", "L0_ffn_b1", "L0_ffn_w2",
        "L0_ffn_b2", "L0_ffn_gamma", "L0_ffn_beta"]


def kernel(**inputs):
    import numpy as _np
    import concourse.bacc as _bacc
    from concourse import mybir as _mybir
    from concourse.bass_utils import run_bass_kernel_spmd as _run

    nc = _bacc.Bacc("TRN2", target_bir_lowering=False, num_devices=1)
    arrays, args = {}, []
    for name in _INS:
        arr = _np.ascontiguousarray(inputs[name])
        arrays[f"in_{name}"] = arr
        args.append(nc.dram_tensor(f"in_{name}", arr.shape, _mybir.dt.from_np(arr.dtype), kind="ExternalInput").ap())
    out = nc.dram_tensor("out_0", (G, N, D), _mybir.dt.float32, kind="ExternalOutput").ap()
    build(nc, *args, out)
    r = _run(nc, [arrays], core_ids=[0])
    return r.results[0]["out_0"]
```

```python
from contextlib import ExitStack

import concourse.bass as bass
from concourse import mybir

F32 = mybir.dt.float32
BF16 = mybir.dt.bfloat16
I32 = mybir.dt.int32
U32 = mybir.dt.uint32
ALU = mybir.AluOpType
ACT = mybir.ActivationFunctionType
X = mybir.AxisListType.X

P = 128
G, N, D = 64, 128, 128
E, F, K = 16, 256, 2
FH = F // P
CH = 8
NC = G // CH
ROUNDS = NC // 2
GR = 4
TOK = G * N
T = 2 * P
RW = D + 4
REGION = TOK + T
TILES = 80
SPARE = TILES - TOK * K // T
RING = 4
TROUNDS = TILES // RING
NOWHERE = 1 << 20
SLOPE = 0.2
EPS = 1e-5
FAR = -1e30
WB = F + FH
assert TILES >= TOK * K // T + E - 1 and TILES <= P


class Steps:

    def __init__(self, eng, sem):
        self.eng, self.sem, self.base, self.n = eng, sem, 0, 0

    def did(self, ins):
        ins.then_inc(self.sem, 1)
        self.n += 1
        return self.n

    def wait(self, n):
        self.eng.wait_ge(self.sem, self.base + n)


def wait(eng, sem, value):
    if not (isinstance(value, int) and value <= 0):
        eng.wait_ge(sem, value)


def rounds(eng, n, body):
    body(0, True, False)
    with eng.Fori(1, n - 1) as r:
        body(r, False, False)
    body(n - 1, False, True)


def build(nc, x, adj, W, a, gate_w, gate_b, w1, b1, w2, b2, gamma, beta, out):
    xs_buf = nc.dram_tensor("expert_rows", (E * REGION + SPARE * T, RW), F32, kind="Internal").ap()
    y_buf = nc.dram_tensor("results", (TOK * K, D), F32, kind="Internal").ap()
    x1_buf = nc.dram_tensor("x1_rows", (NC, P, CH * D), F32, kind="Internal").ap()
    u_buf = nc.dram_tensor("u_rows", (NC, P, CH * D), F32, kind="Internal").ap()
    x_v = x.rearrange("(c k) n d -> c n k d", k=CH)
    adj_v = adj.rearrange("(c k) n m -> c n k m", k=CH)
    out_v = out.rearrange("(c k) n d -> c n k d", k=CH)
    x1_v = x1_buf.rearrange("c n (k d) -> c n k d", k=CH)
    u_v = u_buf.rearrange("c n (k d) -> c n k d", k=CH)
    y_v = y_buf.rearrange("(c k n j) d -> c n k (j d)", k=CH, n=N, j=K)

    with ExitStack() as ctx:
        def sb(name, shape, dt=F32):
            return ctx.enter_context(nc.sbuf_tensor(name, shape, dt))

        def sem(name):
            return ctx.enter_context(nc.semaphore(name))

        def sems(names):
            return [sem(n) for n in names.split()]

        bank = [ctx.enter_context(nc.psum_tensor(f"bank{i}", [P, 512], F32)) for i in range(8)]
        ps_xT, ps_h, ps_pT, ps_pv, ps_uT, ps_gate = (bank[i] for i in (0, 1, 4, 5, 6, 7))
        ps_z = [bank[2], bank[3]]
        ps_rT = [bank[0], bank[5]]
        ps_hid = [bank[1], bank[2]]
        ps_y = [bank[3], bank[4]]

        ident = sb("ident", [P, P])
        ident_b = sb("ident_b", [P, P], BF16)
        ones_b = sb("ones_b", [P, P], BF16)
        before_b = sb("before_b", [P, P], BF16)
        cum48 = sb("cum48", [E, 3 * E], BF16)
        FILL = 8
        empty = sb("empty", [P, FILL, RW])
        W_sb = sb("W_sb", [P, D])
        a_sb = sb("a_sb", [P, 2])
        WT = sb("WT", [P, D])
        v_rep = sb("v_rep", [P, 2, P])
        gw = sb("gw", [P, E])
        gb = sb("gb", [P, E])
        w1_sb = sb("w1_sb", [P, E * WB])
        w2_sb = sb("w2_sb", [P, E * FH * D])
        b2_sb = sb("b2_sb", [P, E, D])
        gamma_sb = sb("gamma_sb", [P, D])
        beta_sb = sb("beta_sb", [P, D])
        iota_e = sb("iota_e", [P, E])
        region = sb("region", [P, E])
        iota_t = sb("iota_t", [P, 1])

        xs = [sb(f"xs{i}", [P, CH, D]) for i in range(2)]
        adj_sb = [sb(f"adj{i}", [P, CH, N], I32) for i in range(2)]
        xn = [sb(f"xn{i}", [P, CH, D]) for i in range(2)]
        x1 = [sb(f"x1{i}", [P, CH, D]) for i in range(2)]
        u = [[sb(f"u{i}_{j}", [P, CH, RW]) for j in range(K)] for i in range(2)]
        xT = [sb(f"xT{i}", [P, GR * N]) for i in range(2)]
        h_sb = [[sb(f"h{i}_{g}", [P, GR * D]) for g in range(2)] for i in range(2)]
        mask = [sb(f"mask{i}", [P, GR * N], BF16) for i in range(2)]
        z02 = [sb(f"z02_{i}", [P, GR * N]) for i in range(2)]
        score = [sb(f"score{i}", [P, GR, N]) for i in range(2)]
        prob = [sb(f"prob{i}", [P, GR, N]) for i in range(2)]
        pT = [sb(f"pT{i}", [P, GR * N]) for i in range(2)]
        uT = [sb(f"uT{i}", [P, GR * N]) for i in range(2)]
        negmax = [sb(f"negmax{i}", [P, GR]) for i in range(2)]
        sums = [sb(f"sums{i}", [P, GR]) for i in range(2)]
        rsum = [sb(f"rsum{i}", [P, GR]) for i in range(2)]
        stat = [sb(f"stat{i}", [P, CH, 6]) for i in range(2)]
        nrm = [sb(f"nrm{i}", [P, 12, CH]) for i in range(2)]
        lg = sb("lg", [P, CH, E])
        l2 = sb("l2", [P, CH, E])
        eq = sb("eq", [P, CH, E])
        cand = sb("cand", [P, CH, E])
        top = sb("top", [P, 8, CH])
        oh = sb("oh", [P, K, CH, E])
        both_b = sb("both_b", [P, CH, E], BF16)
        rank = sb("rank", [P, CH, E])
        picked = sb("picked", [P, K, CH, E])
        pos = [sb(f"pos{i}", [P, K * CH], U32) for i in range(2)]
        seen = sb("seen", [P, E])
        seen_new = sb("seen_new", [P, E])
        seen_b = sb("seen_b", [P, E], BF16)
        wt_all = sb("wt_all", [P, NC * K * CH])
        tiles_i = sb("tiles_i", [E, P], I32)
        tiles_b = sb("tiles_b", [E, P], BF16)
        cums = sb("cums", [P, 3 * E])
        tab = sb("tab", [P, 6])
        tab_cmp = sb("tab_cmp", [P, E])
        tab_mul = sb("tab_mul", [P, E])
        skip = sb("skip", [P, E])
        tab_i = sb("tab_i", [2, P], I32)
        tail_i = sb("tail_i", [P, E], I32)
        rows = [sb(f"rows{i}", [P, 2, RW]) for i in range(RING)]
        place = [sb(f"place{i}", [P, 2], U32) for i in range(RING)]
        y_sb = [sb(f"y_sb{i}", [P, 2, D]) for i in range(RING)]
        rowsT = [sb(f"rowsT{i}", [P, T]) for i in range(2)]
        w1t = [sb(f"w1t{i}", [P, WB]) for i in range(2)]
        hid = [[sb(f"hid{i}_{j}", [P, T]) for j in range(FH)] for i in range(2)]
        yt = [sb(f"yt{i}", [P, CH, K * D]) for i in range(2)]
        wt = [sb(f"wt{i}", [P, K * CH]) for i in range(2)]
        x1b = [sb(f"x1b{i}", [P, CH, D]) for i in range(2)]
        scaled = [sb(f"scaled{i}", [P, CH, D]) for i in range(2)]

        (small_in, loaded, ones_set, ident_set, consts, vec_done, pool_done, prep_done, prep_copied,
         pool_turns) = sems(
            "small_in loaded ones_set ident_set consts vec_done pool_done prep_done prep_copied "
            "pool_turns")
        x_in = sems("x_in0 x_in1")
        adj_in = sems("adj_in0 adj_in1")
        (moments1, guess1, scale1, xn_ready, xT_done, xT_ready, h_done, h_ready, mask_ready, z_done,
         y_ready, max_ready, exp_ready, pT_done, pT_ready, pv_done, x1_done, moments2, guess2,
         u_ready, u2_ready, uT_done, uT_ready, gate_done, both_ready, rank_done, gap_ready,
         odds_ready, pos_ready, seen_ready) = sems(
            "moments1 guess1 scale1 xn_ready xT_done xT_ready h_done h_ready mask_ready z_done "
            "y_ready max_ready exp_ready pT_done pT_ready pv_done x1_done moments2 guess2 "
            "u_ready u2_ready uT_done uT_ready gate_done both_ready rank_done gap_ready "
            "odds_ready pos_ready seen_ready")
        ln_done = sems("ln_done0 ln_done1")
        x1_out = sems("x1_out0 x1_out1")
        u_out = sems("u_out0 u_out1")
        sent = sems("sent0 sent1")
        (emptied, count_done, tiles_ready, cum_done, tab_ready, tab_done, tables_ready,
         tails_ready) = sems(
            "emptied count_done tiles_ready cum_done tab_ready tab_done tables_ready tails_ready")
        rows_in = [sem(f"rows_in{i}") for i in range(RING)]
        y_sent = [sem(f"y_sent{i}") for i in range(RING)]
        (rowsT_done, rowsT_ready, place_ready, w1_ready, hid_done, hid_ready, y_done,
         y_added) = sems("rowsT_done rowsT_ready place_ready w1_ready hid_done hid_ready y_done y_added")
        c_moments, c_guess, c_scale, c_normed, c_scaled, c_added, out_ready = sems(
            "c_moments c_guess c_scale c_normed c_scaled c_added out_ready")
        c_in = sems("c_in0 c_in1")
        x1_in = sems("x1_in0 x1_in1")
        out_done = sems("out_done0 out_done1")

        SMALL, LOADS, POOL_CONSTS, FILLS = 4, 7, 13, SPARE * 2 // FILL
        block = ctx.enter_context(nc.Block())

        @block.sync
        def _(sp):
            def load_chunk(c, par):
                sp.dma_start(xs[par][:], x_v[c]).then_inc(x_in[par], 16)
                sp.dma_start(adj_sb[par][:], adj_v[c]).then_inc(adj_in[par], 16)

            with nc.allow_non_contiguous_dma(reason="vectors with one element to a partition"):
                sp.dma_start(xs[0][:], x_v[0]).then_inc(x_in[0], 16)
                sp.dma_start(W_sb[:], W).then_inc(small_in, 16)
                sp.dma_start(a_sb[:], a.rearrange("r (k o) -> o (r k)", k=2)).then_inc(small_in, 16)
                sp.dma_start(adj_sb[0][:], adj_v[0]).then_inc(adj_in[0], 16)
                sp.dma_start(gw[:], gate_w).then_inc(small_in, 16)
                sp.dma_start(gb[:], gate_b.rearrange("(o e) -> o e", o=1).to_broadcast([P, E])).then_inc(small_in, 16)
                load_chunk(1, 1)
                w1_v = w1_sb[:].rearrange("p (e f) -> p e f", e=E)
                sp.dma_start(w1_v[:, :, 0:F], w1.rearrange("e h f -> h e f")).then_inc(loaded, 16)
                for j in range(FH):
                    sp.dma_start(w1_v[:, :, F + j], b1[:, j * P:(j + 1) * P].rearrange("e p -> p e")).then_inc(loaded, 16)
                sp.dma_start(w2_sb[:].rearrange("p (e j d) -> p e j d", e=E, j=FH),
                             w2.rearrange("e (j p) d -> p e j d", p=P)).then_inc(loaded, 16)
                sp.dma_start(b2_sb[:].rearrange("p e d -> p (e d)"),
                             b2.rearrange("(o e) d -> o (e d)", o=1).to_broadcast([P, E * D])).then_inc(loaded, 16)
                sp.dma_start(gamma_sb[:], gamma.rearrange("(o d) -> o d", o=1).to_broadcast([P, D])).then_inc(loaded, 16)
                sp.dma_start(beta_sb[:], beta.rearrange("(o d) -> o d", o=1).to_broadcast([P, D])).then_inc(loaded, 16)
            sp.wait_ge(pool_done, POOL_CONSTS)
            for n in range(FILLS):
                at = E * REGION + n * FILL * P
                sp.dma_start(xs_buf[at:at + FILL * P, :].rearrange("(p k) w -> p k w", p=P), empty[:]).then_inc(emptied, 16)

            def attention_io(r, first, last):
                for par in range(2):
                    c = 2 * r + par
                    sp.wait_ge(x1_done, 2 * c + 2)
                    sp.dma_start(x1_v[c], x1[par][:]).then_inc(x1_out[par], 16)
                    if not last:
                        load_chunk(c + 2, par)
                    sp.wait_ge(u_ready, 2 * c + 2)
                    sp.dma_start(u_v[c], u[par][0][:, :, 0:D]).then_inc(u_out[par], 16)

            rounds(sp, ROUNDS, attention_io)

            sp.wait_ge(tails_ready, 1)
            with sp.Fori(0, E) as e:
                start = sp.value_load(tail_i[0:1, bass.ds(e, 1)], min_val=0, max_val=E * REGION - T)
                sp.dma_start(xs_buf[bass.ds(start, T), :].rearrange("(p k) w -> p k w", k=2), empty[:, 0:2, :]).then_inc(emptied, 16)
            sp.wait_ge(tables_ready, 1)
            sp.wait_ge(emptied, 16 * (E + FILLS))
            for par in range(2):
                sp.wait_ge(sent[par], ROUNDS * CH * K * 16)

            def load_rows(i, q):
                row = sp.value_load(tab_i[1:2, bass.ds(i, 1)], min_val=0, max_val=E * REGION + (SPARE - 1) * T)
                sp.dma_start(rows[q][:], xs_buf[bass.ds(row, T), :].rearrange("(p k) w -> p k w", k=2)).then_inc(rows_in[q], 16)

            for q in range(RING):
                load_rows(q, q)
            with sp.Fori(0, TROUNDS - 1) as r:
                for q in range(RING):
                    i = RING * r + q
                    sp.wait_ge(rowsT_done, i + 1)
                    sp.wait_ge(place_ready, i + 1)
                    load_rows(i + RING, q)

            def load_results(c, par):
                sp.dma_start(yt[par][:], y_v[c]).then_inc(c_in[par], 16)
                sp.dma_start(u[par][0][:, :, 0:D], u_v[c]).then_inc(c_in[par], 16)

            def load_x1(c, par):
                sp.dma_start(x1[par][:], x1_v[c]).then_inc(x1_in[par], 16)

            for par in range(2):
                sp.wait_ge(x1_out[par], 16 * ROUNDS)
                sp.wait_ge(u_out[par], 16 * ROUNDS)
                load_x1(par, par)
            for q in range(RING):
                sp.wait_ge(y_sent[q], 32 * TROUNDS)
            for par in range(2):
                load_results(par, par)
            with sp.Fori(0, ROUNDS - 1) as r:
                for par in range(2):
                    c = 2 * r + par
                    sp.wait_ge(c_added, c + 1)
                    load_x1(c + 2, par)
                    sp.wait_ge(c_moments, c + 1)
                    load_results(c + 2, par)

        @block.vector
        def _(dve):
            v = nc.vector
            S = Steps(dve, vec_done)

            def bc(ap, shape):
                return ap.to_broadcast(shape)

            def mean_and_var(w):
                m = nrm[w]
                me, qe, mo, qo = (stat[w][:, :, i] for i in (1, 2, 4, 5))
                s = [S.did(v.tensor_tensor(m[:, 2, :], me, mo, ALU.subtract)),
                     S.did(v.tensor_tensor(m[:, 3, :], qe, qo, ALU.add)),
                     S.did(v.tensor_tensor(m[:, 1, :], me, mo, ALU.add))]
                S.wait(s[0])
                S.did(v.scalar_tensor_tensor(out=m[:, 4, :], in0=m[:, 2, :], scalar=0.25, in1=m[:, 2, :],
                                             op0=ALU.mult, op1=ALU.mult))
                S.wait(s[1])
                S.did(v.tensor_scalar(m[:, 5, :], m[:, 3, :], 1.0 / D, EPS, ALU.mult, ALU.add))
                S.wait(s[2])
                s = S.did(v.tensor_scalar(m[:, 0, :], m[:, 1, :], 0.5, None, ALU.mult))
                S.wait(s - 1)
                return v.tensor_tensor(m[:, 6, :], m[:, 4, :], m[:, 5, :], ALU.add)

            def rstd(w):
                m = nrm[w]
                S.wait(S.did(v.tensor_tensor(m[:, 1, :], m[:, 7, :], m[:, 7, :], ALU.mult)))
                S.wait(S.did(v.tensor_tensor(m[:, 2, :], m[:, 1, :], m[:, 6, :], ALU.mult)))
                S.wait(S.did(v.tensor_scalar(m[:, 3, :], m[:, 2, :], -0.5, 1.5, ALU.mult, ALU.add)))
                S.wait(S.did(v.tensor_tensor(m[:, 9, :], m[:, 3, :], m[:, 7, :], ALU.mult)))

            def offset(w):
                return v.scalar_tensor_tensor(out=nrm[w][:, 10, :], in0=nrm[w][:, 0, :], scalar=-1.0,
                                              in1=nrm[w][:, 9, :], op0=ALU.mult, op1=ALU.mult)

            def make_mask(c, par, r):
                dve.wait_ge(adj_in[par], 16 * (r + 1))
                for g in range(2):
                    v.tensor_scalar(mask[g][:], adj_sb[par][:, g * GR:(g + 1) * GR, :].rearrange("p k n -> p (k n)"),
                                    0.0, FAR, ALU.is_equal, ALU.mult).then_inc(mask_ready, 1)

            def first_stat(par, k):
                return S.did(v.bn_stats(stat[0][:, k, :], xs[par][:, k, :]))

            v.memset(ones_b[:], 1.0).then_inc(ones_set, 1)
            S.did(v.memset(seen[:], 0.0))
            S.did(v.memset(seen_b[:], 0.0))
            dve.wait_ge(ident_set, 1)
            v.tensor_copy(ident_b[:], ident[:]).then_inc(consts, 1)
            dve.wait_ge(x_in[0], 16)
            for k in range(CH):
                s = first_stat(0, k)
            S.wait(s)
            mean_and_var(0).then_inc(moments1, 1)
            dve.wait_ge(prep_done, 1)
            v.tensor_copy(WT[:], ps_h[:, 0:D]).then_inc(prep_copied, 1)
            dve.wait_ge(prep_done, 2)
            v.tensor_copy(v_rep[:], bc(ps_h[:, 0:2].unsqueeze(2), [P, 2, P])).then_inc(prep_copied, 1)
            dve.wait_ge(guess1, 1)
            rstd(0)
            offset(0).then_inc(scale1, 1)
            make_mask(0, 0, 0)
            dve.wait_ge(small_in, 16 * SMALL)
            dve.wait_ge(pool_done, POOL_CONSTS)

            def pick(src, at, dst, fill):
                s = S.did(v.tensor_reduce(top[:, at, :], src[:], X, ALU.max))
                fill()
                S.wait(s)
                s = S.did(v.tensor_tensor(eq[:], src[:], bc(top[:, at, :].unsqueeze(2), [P, CH, E]), ALU.is_equal))
                fill()
                S.wait(s)
                s = S.did(v.scalar_tensor_tensor(out=cand[:], in0=eq[:], scalar=-64.0,
                                                 in1=bc(iota_e[:].unsqueeze(1), [P, CH, E]), op0=ALU.mult, op1=ALU.add))
                fill()
                S.wait(s)
                s = S.did(v.tensor_reduce(top[:, at + 1, :], cand[:], X, ALU.min))
                fill()
                S.wait(s)
                S.wait(S.did(v.tensor_tensor(dst, cand[:], bc(top[:, at + 1, :].unsqueeze(2), [P, CH, E]), ALU.is_equal)))

            def gate(c, par, fill):
                dve.wait_ge(gate_done, c + 1)
                S.wait(S.did(v.tensor_tensor(lg[:], ps_gate[:, 0:CH * E].rearrange("p (k e) -> p k e", e=E),
                                             bc(gb[:].unsqueeze(1), [P, CH, E]), ALU.add)))
                pick(lg, 0, oh[:, 0], fill)
                S.wait(S.did(v.scalar_tensor_tensor(out=l2[:], in0=oh[:, 0], scalar=FAR, in1=lg[:],
                                                    op0=ALU.mult, op1=ALU.add)))
                pick(l2, 2, oh[:, 1], fill)
                v.tensor_tensor(both_b[:], oh[:, 0], oh[:, 1], ALU.add).then_inc(both_ready, 1)
                v.tensor_tensor(top[:, 4, :], top[:, 2, :], top[:, 0, :], ALU.subtract).then_inc(gap_ready, 1)
                dve.wait_ge(both_ready, c + 1)
                s = S.did(v.tensor_reduce(seen_new[:], both_b[:].rearrange("p k e -> p e k"), X, ALU.add))
                dve.wait_ge(odds_ready, c + 1)
                S.wait(S.did(v.tensor_scalar(top[:, 6, :], top[:, 5, :], 1.0, None, ALU.add)))
                s = S.did(v.reciprocal(top[:, 7, :], top[:, 6, :]))
                dve.wait_ge(rank_done, c + 1)
                s2 = S.did(v.tensor_tensor(rank[:], ps_gate[:, CH * E:2 * CH * E].rearrange("p (k e) -> p k e", e=E),
                                           bc(region[:].unsqueeze(1), [P, CH, E]), ALU.add))
                S.wait(s)
                S.did(v.tensor_copy(wt_all[:, bass.ds(c * (K * CH), CH)], top[:, 7, :]))
                S.did(v.tensor_tensor(wt_all[:, bass.ds(c * (K * CH) + CH, CH)], top[:, 7, :], top[:, 5, :], ALU.mult))
                S.wait(s2)
                for j in range(K):
                    s = S.did(v.tensor_tensor(picked[:, j], oh[:, j], rank[:], ALU.mult))
                s2 = S.did(v.tensor_tensor(seen[:], seen[:], seen_new[:], ALU.add))
                S.wait(s)
                with nc.allow_low_precision(reason="one whole number and zeros, added in float32"):
                    v.tensor_reduce(pos[par][:], picked[:].rearrange("p j k e -> p (j k) e"), X, ALU.add).then_inc(pos_ready, 1)
                S.wait(s2)
                v.tensor_copy(seen_b[:], seen[:]).then_inc(seen_ready, 1)

            def chunk(c, par, r, prev, ahead):
                for g in range(2):
                    dve.wait_ge(y_ready, 2 * c + g + 1)
                    s = S.did(v.tensor_tensor(score[g][:].rearrange("p k n -> p (k n)"), ps_z[g][:], z02[g][:], ALU.max))
                for g in range(2):
                    S.wait(s - 1 + g)
                    v.tensor_reduce(negmax[g][:], score[g][:], X, ALU.max, negate=True).then_inc(max_ready, 1)
                left = list(range(CH)) if ahead else []
                if ahead:
                    dve.wait_ge(x_in[1 - par], 16 * (r + 1 + par))

                def fill():
                    if left:
                        first_stat(1 - par, left.pop(0))

                if prev:
                    gate(c - 1, 1 - par, fill)
                while left:
                    fill()
                if ahead:
                    S.wait(S.n)
                    mean_and_var(0).then_inc(moments1, 1)
                    make_mask(c + 1, 1 - par, r + par)
                    dve.wait_ge(guess1, c + 2)
                    rstd(0)
                    offset(0).then_inc(scale1, 1)
                wait(dve, x1_out[par], 16 * r)
                for g in range(2):
                    dve.wait_ge(pv_done, 2 * c + g + 1)
                    S.wait(S.did(v.reciprocal(rsum[g][:], sums[g][:])))
                    for k in range(GR):
                        ins = v.scalar_tensor_tensor(out=x1[par][:, g * GR + k, :], in0=ps_pv[:, k * D:(k + 1) * D],
                                                     scalar=rsum[g][:, k:k + 1], in1=xs[par][:, g * GR + k, :],
                                                     op0=ALU.mult, op1=ALU.add)
                    ins.then_inc(x1_done, 1)
                for g in range(2):
                    dve.wait_ge(x1_done, 2 * c + g + 1)
                    for k in range(GR):
                        s = S.did(v.bn_stats(stat[1][:, g * GR + k, :], x1[par][:, g * GR + k, :]))
                S.wait(s)
                mean_and_var(1).then_inc(moments2, 1)
                wait(dve, sent[par], CH * K * 16 * r)
                wait(dve, u_out[par], 16 * r)
                for j in range(K):
                    d = u[par][j][:, :, D].bitcast(I32)
                    S.did(v.tensor_scalar(d, d, float(2 * CH * N * K), None, ALU.add))
                dve.wait_ge(guess2, c + 1)
                rstd(1)
                for k in range(CH):
                    ins = v.tensor_scalar(u[par][0][:, k, 0:D], x1[par][:, k, :], nrm[1][:, 0, k:k + 1],
                                          nrm[1][:, 9, k:k + 1], ALU.subtract, ALU.mult)
                    if k % GR == GR - 1:
                        ins.then_inc(u_ready, 1)

            start = [0, 0]

            def attention(r, first, last):
                if not first and not last:
                    S.base, S.n = start[0] + (r - 1) * PER_ROUND, 0
                if last:
                    S.base, S.n = start[0] + (ROUNDS - 2) * PER_ROUND, 0
                for par in range(2):
                    chunk(2 * r + par, par, r, not first or par == 1, not last or par == 0)
                if first:
                    start[0] = S.base + S.n
                elif not last:
                    assert S.n == PER_ROUND, S.n

            PER_ROUND = 126
            rounds(dve, ROUNDS, attention)
            gate(NC - 1, 1, lambda: None)

            dve.wait_ge(loaded, 16 * LOADS)
            dve.wait_ge(count_done, 1)
            v.tensor_tensor(tail_i[:], ps_gate[:, 0:E], region[:], ALU.add).then_inc(tails_ready, 1)
            S.wait(S.did(v.tensor_scalar(tiles_i[:], ps_h[0:E, 0:P], 1.0 / T, (T - 1) / (2.0 * T), ALU.mult, ALU.add)))
            v.tensor_copy(tiles_b[:], tiles_i[:]).then_inc(tiles_ready, 1)
            dve.wait_ge(cum_done, 1)
            S.wait(S.did(v.tensor_copy(cums[:], ps_h[:, 0:3 * E])))
            S.did(v.tensor_scalar(skip[:], cums[:, 2 * E:], -1.0, float(REGION // T), ALU.mult, ALU.add))
            S.wait(S.did(v.tensor_tensor(tab_cmp[:], bc(iota_t[:], [P, E]), cums[:, 0:E], ALU.is_ge)))
            S.did(v.tensor_tensor(tab_mul[:], tab_cmp[:], skip[:], ALU.mult))
            s = S.did(v.tensor_reduce(tab[:, 2:3], tab_cmp[:], X, ALU.add))
            S.wait(s - 1)
            S.did(v.tensor_reduce(tab[:, 3:4], tab_mul[:], X, ALU.add))
            S.wait(s)
            S.did(v.tensor_scalar(tab[:, 0:1], tab[:, 2:3], float(E - 1), None, ALU.min))
            S.wait(s + 1)
            S.wait(S.did(v.tensor_tensor(tab[:, 4:5], tab[:, 3:4], iota_t[:], ALU.add)))
            v.tensor_scalar(tab[:, 1:2], tab[:, 4:5], float(T), None, ALU.mult).then_inc(tab_ready, 1)
            dve.wait_ge(tab_done, 1)
            v.tensor_copy(tab_i[:], ps_h[0:2, 0:P]).then_inc(tables_ready, 1)
            dve.wait_ge(tables_ready, 1)

            def expert_of(i):
                return dve.value_load(tab_i[0:1, bass.ds(i, 1)], min_val=0, max_val=E - 1)

            def tile_weights(i, q):
                e = expert_of(i)
                wait(dve, hid_ready, FH * (i - 1))
                v.tensor_scalar(w1t[q % 2][:], w1_sb[:, bass.ds(e * WB, WB)], 1.0, None, ALU.mult).then_inc(w1_ready, 1)

            def tiles(r, first, last):
                for q in range(RING):
                    i = RING * r + q
                    if not (last and q == RING - 1):
                        tile_weights(i + 1, q + 1)
                    e = expert_of(i)
                    wait(dve, y_sent[q], 32 * r)
                    dve.wait_ge(rows_in[q], 16 * (r + 1))
                    v.tensor_copy(place[q][:], rows[q][:, :, D].bitcast(U32)).then_inc(place_ready, 1)
                    dve.wait_ge(y_done, i + 1)
                    v.tensor_tensor(y_sb[q][:], ps_y[q % 2][:, 0:T].rearrange("p (k d) -> p k d", k=2),
                                    bc(b2_sb[:, bass.ds(e, 1), :], [P, 2, D]), ALU.add).then_inc(y_added, 1)

            tile_weights(0, 0)
            rounds(dve, TROUNDS, tiles)

            S.base, S.n = S.base + S.n, 0

            def scale(c, par):
                dve.wait_ge(c_normed, c + 1)
                wait(dve, out_ready, c - 1)
                v.tensor_tensor(scaled[par][:], xn[par][:], bc(gamma_sb[:].unsqueeze(1), [P, CH, D]), ALU.mult).then_inc(c_scaled, 1)

            def combine(r, first, last):
                if not first and not last:
                    S.base, S.n = start[0] + (r - 1) * C_ROUND, 0
                if last:
                    S.base, S.n = start[0] + (ROUNDS - 2) * C_ROUND, 0
                for par in range(2):
                    c = 2 * r + par
                    s = S.did(v.tensor_copy(wt[par][:], wt_all[:, bass.ds(c * (K * CH), K * CH)]))
                    S.wait(s)
                    dve.wait_ge(c_in[par], 32 * (r + 1))
                    acc = u[par][1][:, :, 0:D]
                    for j in range(K):
                        for k in range(CH):
                            if j == 1:
                                S.wait(s + 1 + k)
                            S.did(v.scalar_tensor_tensor(out=acc[:, k, :], in0=yt[par][:, k, j * D:(j + 1) * D],
                                                         scalar=wt[par][:, j * CH + k:j * CH + k + 1],
                                                         in1=u[par][0][:, k, 0:D] if j == 0 else acc[:, k, :],
                                                         op0=ALU.mult, op1=ALU.add))
                    for k in range(CH):
                        S.wait(s + 1 + CH + k)
                        S.did(v.bn_stats(stat[1][:, k, :], acc[:, k, :]))
                    S.wait(S.n)
                    mean_and_var(1).then_inc(c_moments, 1)
                    if not first or par == 1:
                        scale(c - 1, 1 - par)
                    dve.wait_ge(c_guess, c + 1)
                    rstd(1)
                    offset(1).then_inc(c_scale, 1)
                if first:
                    start[0] = S.base + S.n
                elif not last:
                    assert S.n == C_ROUND, S.n

            C_ROUND = 2 * (1 + K * CH + CH + 6 + 4)
            rounds(dve, ROUNDS, combine)
            scale(NC - 1, 1)

        @block.scalar
        def _(act):
            s = nc.scalar

            def guess_of(w, n, done):
                s.activation(nrm[w][:, 8, :], nrm[w][:, 6, :], ACT.Ln).then_inc(ln_done[w], 1)
                act.wait_ge(ln_done[w], n)
                s.activation(nrm[w][:, 7, :], nrm[w][:, 8, :], ACT.Exp, scale=-0.5).then_inc(done, 1)

            def norm_rows(dst, src, w):
                for k in range(CH):
                    ins = s.activation(dst[:, k, :], src[:, k, 0:D], ACT.Identity, bias=nrm[w][:, 10, k:k + 1],
                                       scale=nrm[w][:, 9, k:k + 1])
                return ins

            def norm_chunk(c, par):
                act.wait_ge(moments1, c + 1)
                guess_of(0, c + 1, guess1)
                act.wait_ge(scale1, c + 1)
                norm_rows(xn[par], xs[par], 0).then_inc(xn_ready, 1)

            def turned(c):
                for g in range(2):
                    act.wait_ge(xT_done, 2 * c + g + 1)
                    s.activation(xT[g][:], ps_xT[:], ACT.Copy).then_inc(xT_ready, 1)

            def projected(c, par, g):
                act.wait_ge(h_done, 2 * c + g + 1)
                s.activation(h_sb[par][g][:], ps_h[:], ACT.Copy).then_inc(h_ready, 1)
                act.wait_ge(z_done, 2 * c + g + 1)
                s.activation(z02[g][:], ps_z[g][:], ACT.Copy, scale=SLOPE).then_inc(y_ready, 1)

            def u_turned(c):
                for g in range(2):
                    act.wait_ge(uT_done, 2 * c + g + 1)
                    s.activation(uT[g][:], ps_uT[:], ACT.Copy).then_inc(uT_ready, 1)

            def odds(c):
                act.wait_ge(gap_ready, c + 1)
                s.activation(top[:, 5, :], top[:, 4, :], ACT.Exp).then_inc(odds_ready, 1)

            def chunk(c, par, prev, ahead):
                if prev:
                    u_turned(c - 1)
                for g in range(2):
                    act.wait_ge(max_ready, 2 * c + g + 1)
                    for k in range(GR):
                        ins = s.activation(prob[g][:, k, :], score[g][:, k, :], ACT.Exp, bias=negmax[g][:, k:k + 1],
                                           accum_out=sums[g][:, k:k + 1])
                    ins.then_inc(exp_ready, 1)
                for g in range(2):
                    act.wait_ge(pT_done, 2 * c + g + 1)
                    s.activation(pT[g][:], ps_pT[:], ACT.Copy).then_inc(pT_ready, 1)
                    if prev and g == 0:
                        odds(c - 1)
                if ahead:
                    norm_chunk(c + 1, 1 - par)
                    turned(c + 1)
                    projected(c + 1, 1 - par, 0)
                act.wait_ge(moments2, c + 1)
                guess_of(1, c + 1, guess2)
                if ahead:
                    projected(c + 1, 1 - par, 1)
                act.wait_ge(u_ready, 2 * c + 2)
                s.activation(u[par][1][:, :, 0:D], u[par][0][:, :, 0:D], ACT.Copy).then_inc(u2_ready, 1)

            s.preload_act_table_set("natural_log_exp_and_others")
            norm_chunk(0, 0)
            turned(0)
            for g in range(2):
                projected(0, 0, g)

            def attention(r, first, last):
                for par in range(2):
                    chunk(2 * r + par, par, not first or par == 1, not last or par == 0)

            rounds(act, ROUNDS, attention)
            u_turned(NC - 1)
            odds(NC - 1)

            def evacuate(i, q):
                act.wait_ge(rowsT_done, i + 1)
                s.activation(rowsT[q % 2][:], ps_rT[q % 2][:, 0:T], ACT.Copy).then_inc(rowsT_ready, 1)

            def tiles(r, first, last):
                for q in range(RING):
                    i = RING * r + q
                    for j in range(FH):
                        act.wait_ge(hid_done, FH * i + j + 1)
                        s.activation(hid[q % 2][j][:], ps_hid[j][:, 0:T], ACT.Relu,
                                     bias=w1t[q % 2][:, F + j:F + j + 1]).then_inc(hid_ready, 1)
                    if not (last and q == RING - 1):
                        evacuate(i + 1, q + 1)

            evacuate(0, 0)
            rounds(act, TROUNDS, tiles)

            def combine(r, first, last):
                for par in range(2):
                    c = 2 * r + par
                    act.wait_ge(c_moments, c + 1)
                    guess_of(1, NC + c + 1, c_guess)
                    act.wait_ge(c_scale, c + 1)
                    norm_rows(xn[par], u[par][1], 1).then_inc(c_normed, 1)

            rounds(act, ROUNDS, combine)

        @block.tensor
        def _(pe):
            t = nc.tensor

            def mm(out_, lhsT, rhs, start=True, stop=True):
                return t.matmul(out_, lhsT, rhs, start=start, stop=stop)

            pe.wait_ge(ident_set, 1)
            pe.wait_ge(small_in, 16 * SMALL)
            t.transpose(ps_h[:, 0:D], W_sb[:], ident[:]).then_inc(prep_done, 1)
            pe.wait_ge(prep_copied, 1)
            mm(ps_h[:, 0:2], W_sb[:], a_sb[:]).then_inc(prep_done, 1)
            pe.wait_ge(prep_copied, 2)
            pe.wait_ge(consts, 1)
            pe.wait_ge(pool_done, POOL_CONSTS)

            def project(c, par):
                pe.wait_ge(xn_ready, c + 1)
                for g in range(2):
                    wait(pe, xT_ready, 2 * c + g)
                    for k in range(GR):
                        ins = t.transpose(ps_xT[:, k * N:(k + 1) * N], xn[par][:, g * GR + k, :], ident[:])
                    ins.then_inc(xT_done, 1)
                for g in range(2):
                    n = 2 * c + g
                    pe.wait_ge(xT_ready, n + 1)
                    wait(pe, h_ready, n)
                    for k in range(GR):
                        ins = mm(ps_h[:, k * D:(k + 1) * D], xT[g][:, k * N:(k + 1) * N], WT[:])
                    ins.then_inc(h_done, 1)
                    pe.wait_ge(mask_ready, n + 1)
                    mm(ps_z[g][:], v_rep[:, 1, :], xT[g][:], True, False)
                    for k in range(GR):
                        mm(ps_z[g][:, k * N:(k + 1) * N], xT[g][:, k * N:(k + 1) * N], v_rep[:, 0, :], False, False)
                    mm(ps_z[g][:], ident_b[:], mask[g][:], False, True).then_inc(z_done, 1)

            def turn_probs(c, g):
                n = 2 * c + g
                pe.wait_ge(exp_ready, n + 1)
                wait(pe, pT_ready, n)
                for k in range(GR):
                    ins = t.transpose(ps_pT[:, k * N:(k + 1) * N], prob[g][:, k, :], ident[:])
                ins.then_inc(pT_done, 1)

            def aggregate(c, par, g):
                n = 2 * c + g
                pe.wait_ge(pT_ready, n + 1)
                wait(pe, x1_done, n)
                for k in range(GR):
                    ins = mm(ps_pv[:, k * D:(k + 1) * D], pT[g][:, k * N:(k + 1) * N], h_sb[par][g][:, k * D:(k + 1) * D])
                ins.then_inc(pv_done, 1)

            def logits(c, par):
                for g in range(2):
                    n = 2 * c + g
                    pe.wait_ge(u_ready, n + 1)
                    wait(pe, uT_ready, n)
                    for k in range(GR):
                        ins = t.transpose(ps_uT[:, k * N:(k + 1) * N], u[par][0][:, g * GR + k, 0:D], ident[:])
                    ins.then_inc(uT_done, 1)
                wait(pe, pos_ready, c)
                for g in range(2):
                    pe.wait_ge(uT_ready, 2 * c + g + 1)
                    for k in range(GR):
                        at = (g * GR + k) * E
                        ins = mm(ps_gate[:, at:at + E], uT[g][:, k * N:(k + 1) * N], gw[:])
                ins.then_inc(gate_done, 1)

            def ranks(c):
                pe.wait_ge(both_ready, c + 1)
                flat = both_b[:].rearrange("p k e -> p (k e)")
                w = CH * E
                mm(ps_gate[:, w:2 * w], before_b[:], flat, True, False)
                for k in range(1, CH):
                    mm(ps_gate[:, w + k * E:2 * w], ones_b[:], flat[:, 0:(CH - k) * E], False, False)
                wait(pe, seen_ready, c)
                mm(ps_gate[:, w:2 * w], ones_b[:], seen_b[:].unsqueeze(1).to_broadcast([P, CH, E]),
                   False, True).then_inc(rank_done, 1)

            def attention(r, first, last):
                for par in range(2):
                    c = 2 * r + par
                    prev = not first or par == 1
                    if prev:
                        logits(c - 1, 1 - par)
                    turn_probs(c, 0)
                    if prev:
                        ranks(c - 1)
                    turn_probs(c, 1)
                    for g in range(2):
                        aggregate(c, par, g)
                    if not last or par == 0:
                        project(c + 1, 1 - par)

            project(0, 0)
            rounds(pe, ROUNDS, attention)
            logits(NC - 1, 1)
            ranks(NC - 1)

            pe.wait_ge(seen_ready, NC)
            mm(ps_gate[:, 0:E], ones_b[:], seen_b[:])
            mm(ps_h[0:E, 0:P], seen_b[:], ones_b[:]).then_inc(count_done, 1)
            pe.wait_ge(tiles_ready, 1)
            mm(ps_h[:, 0:3 * E], tiles_b[:], cum48[:]).then_inc(cum_done, 1)
            pe.wait_ge(tab_ready, 1)
            t.transpose(ps_h[0:2, 0:P], tab[:, 0:2], ident[:]).then_inc(tab_done, 1)
            pe.wait_ge(tables_ready, 1)

            def turn_rows(i, q, r):
                pe.wait_ge(rows_in[q % RING], 16 * (r + 1))
                wait(pe, rowsT_ready, i - 1)
                for k in range(2):
                    ins = t.transpose(ps_rT[q % 2][:, k * P:(k + 1) * P], rows[q % RING][:, k, 0:D], ident[:])
                ins.then_inc(rowsT_done, 1)

            def tiles(r, first, last):
                for q in range(RING):
                    i = RING * r + q
                    pe.wait_ge(rowsT_ready, i + 1)
                    pe.wait_ge(w1_ready, i + 1)
                    wait(pe, hid_ready, FH * i)
                    for j in range(FH):
                        mm(ps_hid[j][:, 0:T], w1t[q % 2][:, j * P:(j + 1) * P], rowsT[q % 2][:]).then_inc(hid_done, 1)
                    if not (last and q == RING - 1):
                        turn_rows(i + 1, q + 1, r + (q + 1) // RING)
                    e = pe.value_load(tab_i[0:1, bass.ds(i, 1)], min_val=0, max_val=E - 1)
                    wait(pe, y_added, i - 1)
                    for j in range(FH):
                        pe.wait_ge(hid_ready, FH * i + j + 1)
                        for k in range(2):
                            ins = mm(ps_y[q % 2][:, k * D:(k + 1) * D], hid[q % 2][j][:, k * P:(k + 1) * P],
                                     w2_sb[:, bass.ds(e * (FH * D) + j * D, D)], j + k == 0, j + k == FH)
                    ins.then_inc(y_done, 1)

            turn_rows(0, 0, 0)
            rounds(pe, TROUNDS, tiles)

        @block.gpsimd
        def _(pool):
            p = nc.gpsimd
            S = Steps(pool, pool_done)
            S.wait(S.did(p.memset(ident[:], 1.0)))
            p.affine_select(ident[:], ident[:], pattern=[[-1, P]], compare_op=ALU.is_equal, fill=0.0, base=0,
                            channel_multiplier=1).then_inc(ident_set, 1)
            S.did(p.memset(cum48[:], 1.0))
            for par in range(2):
                for j in range(K):
                    p.memset(u[par][j][:, :, D:RW], 0.0)
            p.memset(empty[:], 0.0)
            S.wait(S.did(p.memset(before_b[:], 1.0)))
            S.did(p.affine_select(before_b[:], before_b[:], pattern=[[1, P]], compare_op=ALU.is_gt, fill=0.0, base=0,
                                  channel_multiplier=-1))
            for n, op in enumerate((ALU.is_ge, ALU.is_gt, ALU.is_equal)):
                S.did(p.affine_select(cum48[:, n * E:(n + 1) * E], cum48[:, n * E:(n + 1) * E], pattern=[[1, E]],
                                      compare_op=op, fill=0.0, base=0, channel_multiplier=-1))
            S.did(p.iota(iota_e[:], pattern=[[1, E]], base=0, channel_multiplier=0, allow_small_or_imprecise_dtypes=True))
            S.did(p.iota(region[:], pattern=[[REGION, E]], base=0, channel_multiplier=0, allow_small_or_imprecise_dtypes=True))
            S.did(p.iota(iota_t[:], pattern=[[0, 1]], base=0, channel_multiplier=1, allow_small_or_imprecise_dtypes=True))
            for par in range(2):
                for j in range(K):
                    ins = p.iota(u[par][j][:, :, D].bitcast(I32), pattern=[[N * K, CH]],
                                 base=par * CH * N * K + j - 2 * CH * N * K, channel_multiplier=K)
            S.did(ins)
            S.did(p.iota(empty[:, :, D].bitcast(I32), pattern=[[0, FILL]], base=NOWHERE, channel_multiplier=0))
            S.did(p.memset(empty[:, :, D + 1:], 0.0))

            def send(r, first, last):
                for par in range(2):
                    pool.wait_ge(pos_ready, 2 * r + par + 1)
                    pool.wait_ge(u2_ready, 2 * r + par + 1)
                    pool.sem_inc(pool_turns, 1)
                    for j in range(K):
                        for k in range(CH):
                            p.indirect_dma_start(xs_buf, bass.IndirectOffsetOnAxis(ap=pos[par][:, j * CH + k:j * CH + k + 1], axis=0),
                                                 u[par][j][:, k, :], None).then_inc(sent[par], 16)

            rounds(pool, ROUNDS, send)

            def send_results(r, first, last):
                for q in range(RING):
                    pool.wait_ge(y_added, RING * r + q + 1)
                    pool.sem_inc(pool_turns, 1)
                    for k in range(2):
                        p.indirect_dma_start(y_buf, bass.IndirectOffsetOnAxis(ap=place[q][:, k:k + 1], axis=0),
                                             y_sb[q][:, k, :], None, bounds_check=TOK * K - 1,
                                             oob_is_err=False).then_inc(y_sent[q], 16)

            rounds(pool, TROUNDS, send_results)

            def combine(r, first, last):
                for par in range(2):
                    c = 2 * r + par
                    pool.wait_ge(x1_in[par], 16 * (r + 1))
                    p.tensor_tensor(x1b[par][:], x1[par][:], beta_sb[:].unsqueeze(1).to_broadcast([P, CH, D]),
                                    ALU.add).then_inc(c_added, 1)
                    wait(pool, out_done[par], 16 * r)
                    pool.wait_ge(c_added, c + 1)
                    pool.wait_ge(c_scaled, c + 1)
                    p.tensor_tensor(xs[par][:], scaled[par][:], x1b[par][:], ALU.add).then_inc(out_ready, 1)
                    pool.wait_ge(out_ready, c + 1)
                    pool.sem_inc(pool_turns, 1)
                    pool.dma_start(out_v[c], xs[par][:]).then_inc(out_done[par], 16)

            rounds(pool, ROUNDS, combine)
            for par in range(2):
                pool.wait_ge(out_done[par], 16 * ROUNDS)


_INS = ["x", "adj", "L0_gnn_W", "L0_gnn_a", "L0_ffn_gate_w", "L0_ffn_gate_b", "L0_ffn_w1", "L0_ffn_b1", "L0_ffn_w2",
        "L0_ffn_b2", "L0_ffn_gamma", "L0_ffn_beta"]


def kernel(**inputs):
    import numpy as _np
    import concourse.bacc as _bacc
    from concourse import mybir as _mybir
    from concourse.bass_utils import run_bass_kernel_spmd as _run

    nc = _bacc.Bacc("TRN2", target_bir_lowering=False, num_devices=1)
    arrays, args = {}, []
    for name in _INS:
        arr = _np.ascontiguousarray(inputs[name])
        arrays[f"in_{name}"] = arr
        args.append(nc.dram_tensor(f"in_{name}", arr.shape, _mybir.dt.from_np(arr.dtype), kind="ExternalInput").ap())
    out = nc.dram_tensor("out_0", (G, N, D), _mybir.dt.float32, kind="ExternalOutput").ap()
    build(nc, *args, out)
    r = _run(nc, [arrays], core_ids=[0])
    return r.results[0]["out_0"]
```

```python
from contextlib import ExitStack

import concourse.bass as bass
from concourse import mybir

F32 = mybir.dt.float32
BF16 = mybir.dt.bfloat16
I32 = mybir.dt.int32
U32 = mybir.dt.uint32
ALU = mybir.AluOpType
ACT = mybir.ActivationFunctionType
X = mybir.AxisListType.X

P = 128
G, N, D = 64, 128, 128
E, F, K = 16, 256, 2
FH = F // P
CH = 8
NC = G // CH
ROUNDS = NC // 2
GR = 4
SHARE = 2
TOK = G * N
T = 2 * P
RW = D + 4
REGION = TOK + T
TILES = TOK * K // T + E - 1
SPARE = TILES - TOK * K // T
RING = 8
YRING = 4
TROUNDS = -(-TILES // RING)
LAST = TILES - RING * (TROUNDS - 1)
NOWHERE = 1 << 20
SLOPE = 0.2
EPS = 1e-5
FAR = -1e30
WB = F + FH + D
assert TILES <= P and LAST > 2


class Steps:

    def __init__(self, eng, sem):
        self.eng, self.sem, self.base, self.n = eng, sem, 0, 0

    def did(self, ins):
        ins.then_inc(self.sem, 1)
        self.n += 1
        return self.n

    def wait(self, n):
        self.eng.wait_ge(self.sem, self.base + n)


def wait(eng, sem, value):
    if not (isinstance(value, int) and value <= 0):
        eng.wait_ge(sem, value)


def rounds(eng, n, body):
    body(0, True, False)
    with eng.Fori(1, n - 1) as r:
        body(r, False, False)
    body(n - 1, False, True)


def build(nc, x, adj, W, a, gate_w, gate_b, w1, b1, w2, b2, gamma, beta, out):
    xs_buf = nc.dram_tensor("expert_rows", (E * REGION + SPARE * T, RW), F32, kind="Internal").ap()
    y_buf = nc.dram_tensor("results", (TOK * K, D), F32, kind="Internal").ap()
    u_buf = nc.dram_tensor("u_rows", (NC, P, CH * D), F32, kind="Internal").ap()
    x_v = x.rearrange("(c k) n d -> c n k d", k=CH)
    adj_v = adj.rearrange("(c k) n m -> c n k m", k=CH)
    out_v = out.rearrange("(c k) n d -> c n k d", k=CH)
    u_v = u_buf.rearrange("c n (k d) -> c n k d", k=CH)
    y_v = y_buf.rearrange("(c k n j) d -> c n k (j d)", k=CH, n=N, j=K)

    with ExitStack() as ctx:
        def sb(name, shape, dt=F32):
            return ctx.enter_context(nc.sbuf_tensor(name, shape, dt))

        def sem(name):
            return ctx.enter_context(nc.semaphore(name))

        def sems(names):
            return [sem(n) for n in names.split()]

        bank = [ctx.enter_context(nc.psum_tensor(f"bank{i}", [P, 512], F32)) for i in range(8)]
        ps_u, ps_h, ps_gate = (bank[i] for i in (0, 1, 7))
        ps_xT = [ps_h, bank[5]]
        ps_pT = [bank[4], ps_u]
        ps_hg = [ps_h, bank[4]]
        ps_pv = [bank[5], bank[6]]
        ps_z = [bank[2], bank[3]]
        ps_rT = [bank[0], bank[5]]
        ps_hid = [bank[1], bank[2]]
        ps_y = [bank[3], bank[4]]

        ident = sb("ident", [P, P])
        ident_b = sb("ident_b", [P, P], BF16)
        ones_b = sb("ones_b", [P, P], BF16)
        before_b = sb("before_b", [P, P], BF16)
        cum48 = sb("cum48", [E, 3 * E], BF16)
        FILL = 2
        empty = sb("empty", [P, FILL, RW])
        W_sb = sb("W_sb", [P, D])
        a_sb = sb("a_sb", [P, 2])
        WT = sb("WT", [P, D])
        v_rep = sb("v_rep", [P, 2, P])
        gw = sb("gw", [P, E])
        gb = sb("gb", [P, E])
        w1_sb = sb("w1_sb", [P, E * WB])
        w2_sb = sb("w2_sb", [P, E * FH * D])
        gamma_sb = sb("gamma_sb", [P, D])
        beta_sb = sb("beta_sb", [P, D])
        iota_e = sb("iota_e", [P, E])
        region = sb("region", [P, E])
        iota_t = sb("iota_t", [P, 1])

        xs_mem, adj_mem = (sb(name, [P, 2 * CH * D]) for name in ("xs", "adj"))
        xs, adj_sb = ([mem[:, i * CH * D:(i + 1) * CH * D].rearrange("p (k d) -> p k d", k=CH) for i in range(2)]
                      for mem in (xs_mem, adj_mem))
        adj_sb = [one.bitcast(I32) for one in adj_sb]
        x1_all = sb("x1_all", [P, NC * CH, D])
        xn = [sb(f"xn{i}", [P, CH, D]) for i in range(2)]
        x1 = [sb(f"x1{i}", [P, CH, D]) for i in range(2)]
        u = [[sb(f"u{i}_{j}", [P, CH, RW]) for j in range(K)] for i in range(2)]
        xT = [sb(f"xT{i}", [P, GR * N]) for i in range(2)]
        h_sb = [[sb(f"h{i}_{g}", [P, GR * D]) for g in range(2)] for i in range(2)]
        mask = [sb(f"mask{i}", [P, GR * N], BF16) for i in range(2)]
        z02 = [sb(f"z02_{i}", [P, GR * N]) for i in range(2)]
        score = [sb(f"score{i}", [P, GR, N]) for i in range(2)]
        prob = [sb(f"prob{i}", [P, GR, N]) for i in range(2)]
        pT = [sb(f"pT{i}", [P, GR * N]) for i in range(2)]
        uT = [sb(f"uT{i}", [P, GR * N]) for i in range(2)]
        negmax = [sb(f"negmax{i}", [P, GR]) for i in range(2)]
        sums, rsum = (sb(name, [P, CH]) for name in ("sums", "rsum"))
        stat = sb("stat", [P, 2, CH, 6])
        nrm = sb("nrm", [P, 11, 2, CH])
        lg = sb("lg", [P, CH, E])
        l2 = sb("l2", [P, CH, E])
        eq = sb("eq", [P, CH, E])
        cand = sb("cand", [P, CH, E])
        top = sb("top", [P, 8, CH])
        oh = sb("oh", [P, K, CH, E])
        both_b = sb("both_b", [P, CH, E], BF16)
        rank = sb("rank", [P, CH, E])
        picked = sb("picked", [P, K, CH, E])
        pos = [sb(f"pos{i}", [P, K * CH], U32) for i in range(2)]
        seen = sb("seen", [P, E])
        seen_new = sb("seen_new", [P, E])
        seen_b = sb("seen_b", [P, E], BF16)
        tiles_i = sb("tiles_i", [E, P], I32)
        tiles_b = sb("tiles_b", [E, P], BF16)
        cums = sb("cums", [P, 3 * E])
        tab = sb("tab", [P, 6])
        tab_cmp = sb("tab_cmp", [P, E])
        tab_mul = sb("tab_mul", [P, E])
        skip = sb("skip", [P, E])
        tab_i = sb("tab_i", [2, P], I32)
        tail_i = sb("tail_i", [P, E], I32)
        rows = [sb(f"rows{i}", [P, 2, RW]) for i in range(RING)]
        y_sb = [sb(f"y_sb{i}", [P, 2, D]) for i in range(YRING)]
        rowsT = [sb(f"rowsT{i}", [P, T]) for i in range(2)]
        wts = [sb(f"wts{i}", [P, WB]) for i in range(YRING)]
        hid = [[h_sb[i][j][:, 0:T] for j in range(FH)] for i in range(2)]
        yt = [mem[:].rearrange("p (k w) -> p k w", k=CH) for mem in (xs_mem, adj_mem)]

        (small_in, loaded, ident_set, consts, vec_done, pool_done, prep_done, prep_copied,
         pool_turns) = sems(
            "small_in loaded ident_set consts vec_done pool_done prep_done prep_copied "
            "pool_turns")
        x_in = [sems("x_in0_0 x_in0_1"), sems("x_in1_0 x_in1_1")]
        adj_in = sems("adj_in0 adj_in1")
        (moments, guess, scale1, xT_done, xT_ready, h_done, h_ready, mask_ready, z_done,
         y_ready, max_ready, exp_ready, pT_done, pT_ready, pv_done, x1_done,
         u_ready, u2_ready, uT_done, uT_ready, gate_done, both_ready, rank_done, gap_ready,
         odds_ready, pos_ready, seen_ready) = sems(
            "moments guess scale1 xT_done xT_ready h_done h_ready mask_ready z_done "
            "y_ready max_ready exp_ready pT_done pT_ready pv_done x1_done "
            "u_ready u2_ready uT_done uT_ready gate_done both_ready rank_done gap_ready "
            "odds_ready pos_ready seen_ready")
        xn_ready = sems("xn_ready0 xn_ready1")
        ln_done = sem("ln_done")
        x1_kept = sems("x1_kept0 x1_kept1")
        u_out = sems("u_out0 u_out1")
        sent = sems("sent0 sent1")
        emptied = sems("emptied0 emptied1")
        (count_done, tiles_ready, cum_done, tab_ready, tab_done, tables_ready,
         tails_ready) = sems(
            "count_done tiles_ready cum_done tab_ready tab_done tables_ready tails_ready")
        rows_in = [sem(f"rows_in{i}") for i in range(RING)]
        y_sent = [sem(f"y_sent{i}") for i in range(RING)]
        (rowsT_done, rowsT_ready, wts_ready, y_biased, hid_done, hid_ready, y_done,
         y_added) = sems("rowsT_done rowsT_ready wts_ready y_biased hid_done hid_ready y_done y_added")
        c_first, c_summed, last_ready, c_moments, c_guess, c_scale, c_normed, c_scaled, out_ready, beta_added = sems(
            "c_first c_summed last_ready c_moments c_guess c_scale c_normed c_scaled out_ready beta_added")
        c_in = sems("c_in0 c_in1")
        out_done = sems("out_done0 out_done1")

        FIRST, SECOND = slice(0, 1), slice(1, 2)
        SMALL, LOADS, POOL_CONSTS, FILLS = 4, 7, 13, SPARE * 2 // FILL
        block = ctx.enter_context(nc.Block())

        def empty_tails(eng, half):
            with eng.Fori(half * (E // 2), (half + 1) * (E // 2)) as e:
                start = eng.value_load(tail_i[0:1, bass.ds(e, 1)], min_val=0, max_val=E * REGION - T)
                eng.dma_start(xs_buf[bass.ds(start, T), :].rearrange("(p k) w -> p k w", k=2), empty[:]).then_inc(emptied[half], 16)

        @block.sync
        def _(sp):
            def load_x(c, par, g):
                half = slice(g * GR, (g + 1) * GR)
                sp.dma_start(xs[par][:, half], x_v[c][:, half]).then_inc(x_in[par][g], 16)

            def load_adj(c, par):
                sp.dma_start(adj_sb[par][:], adj_v[c]).then_inc(adj_in[par], 16)

            with nc.allow_non_contiguous_dma(reason="vectors with one element to a partition"):
                for g in range(2):
                    load_x(0, 0, g)
                sp.dma_start(W_sb[:], W).then_inc(small_in, 16)
                sp.dma_start(a_sb[:], a.rearrange("r (k o) -> o (r k)", k=2)).then_inc(small_in, 16)
                sp.dma_start(adj_sb[0][:], adj_v[0]).then_inc(adj_in[0], 16)
                sp.dma_start(gw[:], gate_w).then_inc(small_in, 16)
                sp.dma_start(gb[:], gate_b.rearrange("(o e) -> o e", o=1).to_broadcast([P, E])).then_inc(small_in, 16)
                for g in range(2):
                    load_x(1, 1, g)
                load_adj(1, 1)
                w1_v = w1_sb[:].rearrange("p (e f) -> p e f", e=E)
                sp.dma_start(w1_v[:, :, 0:F], w1.rearrange("e h f -> h e f")).then_inc(loaded, 16)
                for j in range(FH):
                    sp.dma_start(w1_v[:, :, F + j], b1[:, j * P:(j + 1) * P].rearrange("e p -> p e")).then_inc(loaded, 16)
                sp.dma_start(gamma_sb[:], gamma.rearrange("(o d) -> o d", o=1).to_broadcast([P, D])).then_inc(loaded, 16)
                sp.dma_start(beta_sb[:], beta.rearrange("(o d) -> o d", o=1).to_broadcast([P, D])).then_inc(loaded, 16)

            def store_u(c, par):
                sp.wait_ge(u_ready, 2 * c + 2)
                sp.dma_start(u_v[c], u[par][0][:, :, 0:D]).then_inc(u_out[par], 16)

            def attention_io(r, first, last):
                for par in range(2):
                    c = 2 * r + par
                    if not first or par == 1:
                        store_u(c - 1, 1 - par)
                    for g in range(2):
                        sp.wait_ge(x1_done, 2 * c + g + 1)
                        if not last:
                            load_x(c + 2, par, g)
                    if not last:
                        load_adj(c + 2, par)
                    sp.dma_start(x1_all[:, bass.ds(c * CH, CH), :], x1[par][:]).then_inc(x1_kept[par], 16)
                if first:
                    sp.dma_start(w2_sb[:].rearrange("p (e j d) -> p e j d", e=E, j=FH),
                                 w2.rearrange("e (j p) d -> p e j d", p=P)).then_inc(loaded, 16)
                    sp.dma_start(w1_v[:, :, F + FH:], b2.rearrange("(o e) d -> o e d", o=1).to_broadcast([P, E, D])).then_inc(loaded, 16)

            rounds(sp, ROUNDS, attention_io)
            sp.wait_ge(pool_done, POOL_CONSTS)
            for n in range(FILLS):
                at = E * REGION + n * FILL * P
                sp.dma_start(xs_buf[at:at + FILL * P, :].rearrange("(p k) w -> p k w", p=P), empty[:]).then_inc(emptied[0], 16)
            store_u(NC - 1, 1)

            sp.wait_ge(tails_ready, 1)
            empty_tails(sp, 0)
            sp.wait_ge(tables_ready, 1)
            for half in range(2):
                sp.wait_ge(emptied[half], 16 * (E // 2 + (FILLS if half == 0 else 0)))

            def row_of(i):
                return sp.value_load(tab_i[1:2, bass.ds(i, 1)], min_val=0, max_val=E * REGION + (SPARE - 1) * T)

            def load_rows(i, q, row=None):
                row = row_of(i) if row is None else row
                sp.dma_start(rows[q][:], xs_buf[bass.ds(row, T), :].rearrange("(p k) w -> p k w", k=2)).then_inc(rows_in[q], 16)

            row = row_of(0)
            for par in range(2):
                sp.wait_ge(sent[par], ROUNDS * CH * K * 16)
            load_rows(0, 0, row)
            for q in range(1, RING):
                load_rows(q, q)

            def reload(r, tiles):
                for q in range(tiles):
                    i = RING * r + q
                    sp.wait_ge(rowsT_done, i + 1)
                    sp.wait_ge(y_sent[q], 32 * (r + 1))
                    load_rows(i + RING, q)

            with sp.Fori(0, TROUNDS - 2) as r:
                reload(r, RING)
            reload(TROUNDS - 2, LAST)

            def load_results(c, par):
                sp.dma_start(yt[par][:], y_v[c]).then_inc(c_in[par], 16)

            def load_u(c, par):
                sp.dma_start(u[par][0][:, :, 0:D], u_v[c]).then_inc(c_in[par], 16)

            def store(c, par):
                sp.wait_ge(out_ready, c + 1)
                sp.dma_start(out_v[c], xn[par][:]).then_inc(out_done[par], 16)

            for par in range(2):
                sp.wait_ge(u_out[par], 16 * ROUNDS)
                load_u(par, par)
            for q in range(RING):
                sp.wait_ge(y_sent[q], 32 * (TROUNDS - (q >= LAST)))
            for par in range(2):
                load_results(par, par)

            def combine_io(r, first, last):
                for par in range(2):
                    c = 2 * r + par
                    if not last:
                        sp.wait_ge(c_summed, 2 * c + 2)
                        load_results(c + 2, par)
                        load_u(c + 2, par)
                    if not first or par == 1:
                        store(c - 1, 1 - par)

            rounds(sp, ROUNDS, combine_io)
            for g in range(2):
                sp.wait_ge(last_ready, g + 1)
                half = slice(g * GR, (g + 1) * GR)
                sp.dma_start(out_v[NC - 1][:, half, :], xn[1][:, half]).then_inc(out_done[1], 16)
            for par in range(2):
                sp.wait_ge(out_done[par], 16 * (ROUNDS + par))

        @block.vector
        def _(dve):
            v = nc.vector
            S = Steps(dve, vec_done)

            def bc(ap, shape):
                return ap.to_broadcast(shape)

            def mean_and_var(w):
                m = nrm[:, :, w]
                me, qe, mo, qo = (stat[:, w, :, i] for i in (1, 2, 4, 5))
                s = [S.did(v.tensor_tensor(m[:, 2], me, mo, ALU.subtract)),
                     S.did(v.tensor_tensor(m[:, 3], qe, qo, ALU.add)),
                     S.did(v.tensor_tensor(m[:, 1], me, mo, ALU.add))]
                S.wait(s[0])
                S.did(v.scalar_tensor_tensor(out=m[:, 4], in0=m[:, 2], scalar=0.25, in1=m[:, 2],
                                             op0=ALU.mult, op1=ALU.mult))
                S.wait(s[1])
                S.did(v.tensor_scalar(m[:, 5], m[:, 3], 1.0 / D, EPS, ALU.mult, ALU.add))
                S.wait(s[2])
                s = S.did(v.tensor_scalar(m[:, 0], m[:, 1], 0.5, None, ALU.mult))
                S.wait(s - 1)
                return v.tensor_tensor(m[:, 6], m[:, 4], m[:, 5], ALU.add)

            def rstd(w):
                m = nrm[:, :, w]
                S.wait(S.did(v.tensor_tensor(m[:, 1], m[:, 7], m[:, 7], ALU.mult)))
                S.wait(S.did(v.tensor_tensor(m[:, 2], m[:, 1], m[:, 6], ALU.mult)))
                S.wait(S.did(v.tensor_scalar(m[:, 3], m[:, 2], -0.5, 1.5, ALU.mult, ALU.add)))
                S.wait(S.did(v.tensor_tensor(m[:, 9], m[:, 3], m[:, 7], ALU.mult)))

            def offset(w):
                return v.scalar_tensor_tensor(out=nrm[:, 10, w], in0=nrm[:, 0, w], scalar=-1.0,
                                              in1=nrm[:, 9, w], op0=ALU.mult, op1=ALU.mult)

            def stats_of_x(par):
                for k in range(CH):
                    if k % GR == 0:
                        dve.wait_ge(x_in[par][k // GR], 16)
                    S.did(v.bn_stats(stat[:, 0, k, :], xs[par][:, k, :]))

            def make_mask(c, par, r):
                dve.wait_ge(adj_in[par], 16 * (r + 1))
                for g in range(2):
                    v.tensor_scalar(mask[g][:], adj_sb[par][:, g * GR:(g + 1) * GR, :].rearrange("p k n -> p (k n)"),
                                    0.0, FAR, ALU.is_equal, ALU.mult).then_inc(mask_ready, 1)

            def norm_first_rows(par):
                for k in range(SHARE):
                    ins = v.tensor_scalar(xn[par][:, k, :], xs[par][:, k, :], nrm[:, 0, 0, k:k + 1],
                                          nrm[:, 9, 0, k:k + 1], ALU.subtract, ALU.mult)
                ins.then_inc(xn_ready[0], 1)

            v.memset(ones_b[:], 1.0)
            S.did(v.memset(seen[:], 0.0))
            S.did(v.memset(seen_b[:], 0.0))
            dve.wait_ge(ident_set, 1)
            v.tensor_copy(ident_b[:], ident[:]).then_inc(consts, 1)
            stats_of_x(0)
            S.wait(S.n)
            mean_and_var(FIRST).then_inc(moments, 1)
            dve.wait_ge(prep_done, 1)
            v.tensor_copy(WT[:], ps_gate[:, 0:D]).then_inc(prep_copied, 1)
            dve.wait_ge(guess, 1)
            rstd(FIRST)
            offset(FIRST).then_inc(scale1, 1)
            norm_first_rows(0)
            dve.wait_ge(prep_done, 2)
            v.tensor_copy(v_rep[:], bc(ps_gate[:, 0:2].unsqueeze(2), [P, 2, P])).then_inc(prep_copied, 1)
            make_mask(0, 0, 0)
            stats_of_x(1)
            S.wait(S.n)
            mean_and_var(FIRST).then_inc(moments, 1)
            dve.wait_ge(small_in, 16 * SMALL)
            dve.wait_ge(pool_done, POOL_CONSTS)

            def pick(src, at, dst, fill):
                s = S.did(v.tensor_reduce(top[:, at, :], src[:], X, ALU.max))
                fill()
                S.wait(s)
                s = S.did(v.tensor_tensor(eq[:], src[:], bc(top[:, at, :].unsqueeze(2), [P, CH, E]), ALU.is_equal))
                fill()
                S.wait(s)
                s = S.did(v.scalar_tensor_tensor(out=cand[:], in0=eq[:], scalar=-64.0,
                                                 in1=bc(iota_e[:].unsqueeze(1), [P, CH, E]), op0=ALU.mult, op1=ALU.add))
                fill()
                S.wait(s)
                s = S.did(v.tensor_reduce(top[:, at + 1, :], cand[:], X, ALU.min))
                fill()
                S.wait(s)
                S.wait(S.did(v.tensor_tensor(dst, cand[:], bc(top[:, at + 1, :].unsqueeze(2), [P, CH, E]), ALU.is_equal)))

            def gate(c, fill):
                dve.wait_ge(gate_done, c + 1)
                S.wait(S.did(v.tensor_tensor(lg[:], ps_gate[:, 0:CH * E].rearrange("p (k e) -> p k e", e=E),
                                             bc(gb[:].unsqueeze(1), [P, CH, E]), ALU.add)))
                pick(lg, 0, oh[:, 0], fill)
                S.wait(S.did(v.scalar_tensor_tensor(out=l2[:], in0=oh[:, 0], scalar=FAR, in1=lg[:],
                                                    op0=ALU.mult, op1=ALU.add)))
                pick(l2, 2, oh[:, 1], fill)
                v.tensor_tensor(both_b[:], oh[:, 0], oh[:, 1], ALU.add).then_inc(both_ready, 1)
                v.tensor_tensor(top[:, 4, :], top[:, 2, :], top[:, 0, :], ALU.subtract).then_inc(gap_ready, 1)
                dve.wait_ge(both_ready, c + 1)
                S.did(v.tensor_reduce(seen_new[:], both_b[:].rearrange("p k e -> p e k"), X, ALU.add))

            def odds_sum(c):
                dve.wait_ge(odds_ready, c + 1)
                return S.did(v.tensor_scalar(top[:, 6, :], top[:, 5, :], 1.0, None, ALU.add))

            def rank_in_all(c):
                dve.wait_ge(rank_done, c + 1)
                return S.did(v.tensor_tensor(rank[:], ps_gate[:, CH * E:2 * CH * E].rearrange("p (k e) -> p k e", e=E),
                                             bc(region[:].unsqueeze(1), [P, CH, E]), ALU.add))

            def places(par, c, s_odds, s_rank):
                S.wait(s_odds)
                s = S.did(v.reciprocal(top[:, 7, :], top[:, 6, :]))
                S.wait(s_rank)
                S.did(v.tensor_tensor(picked[:].rearrange("p j k e -> p j (k e)"), oh[:].rearrange("p j k e -> p j (k e)"),
                                      bc(rank[:].rearrange("p k e -> p (k e)").unsqueeze(1), [P, K, CH * E]), ALU.mult))
                S.wait(s)
                S.did(v.tensor_copy(u[par][0][:, :, D + 1], top[:, 7, :]))
                S.did(v.tensor_tensor(u[par][1][:, :, D + 1], top[:, 7, :], top[:, 5, :], ALU.mult))
                s = s + 1
                s2 = S.did(v.tensor_tensor(seen[:], seen[:], seen_new[:], ALU.add))
                S.wait(s)
                with nc.allow_low_precision(reason="one whole number and zeros, added in float32"):
                    v.tensor_reduce(pos[par][:], picked[:].rearrange("p j k e -> p (j k) e"), X, ALU.add).then_inc(pos_ready, 1)
                S.wait(s2)
                v.tensor_copy(seen_b[:], seen[:]).then_inc(seen_ready, 1)

            def norm_u(c, par, r):
                wait(dve, sent[par], CH * K * 16 * r)
                wait(dve, u_out[par], 16 * r)
                for j in range(K):
                    d = u[par][j][:, :, D].bitcast(I32)
                    S.did(v.tensor_scalar(d, d, float(2 * CH * N * K), None, ALU.add))
                for k in range(CH):
                    ins = v.tensor_scalar(u[par][0][:, k, 0:D], x1[par][:, k, :], nrm[:, 0, 1, k:k + 1],
                                          nrm[:, 9, 1, k:k + 1], ALU.subtract, ALU.mult)
                    if k % GR == GR - 1:
                        ins.then_inc(u_ready, 1)

            def chunk(c, par, r, before, prev, ahead, beyond):
                part = []
                for g in range(2):
                    dve.wait_ge(y_ready, 2 * c + g + 1)
                    s = S.did(v.tensor_tensor(score[g][:].rearrange("p k n -> p (k n)"), ps_z[g][:], z02[g][:], ALU.max))
                    if before:
                        part.append((odds_sum, rank_in_all)[g](c - 2))
                    S.wait(s)
                    v.tensor_reduce(negmax[g][:], score[g][:], X, ALU.max, negate=True).then_inc(max_ready, 1)
                if before:
                    places(par, c - 2, *part)
                w = slice(0 if ahead else 1, 2 if prev else 1)
                dve.wait_ge(guess, c + 2)
                rstd(w)
                if ahead:
                    offset(FIRST).then_inc(scale1, 1)
                if prev:
                    norm_u(c - 1, 1 - par, r - 1 + par)
                if ahead:
                    norm_first_rows(1 - par)
                dve.wait_ge(exp_ready, 2 * c + 2)
                reciprocal = S.did(v.reciprocal(rsum[:], sums[:]))
                if ahead:
                    make_mask(c + 1, 1 - par, r + par)
                S.wait(reciprocal)
                wait(dve, x1_kept[par], 16 * r)
                for g in range(2):
                    dve.wait_ge(pv_done, 2 * c + g + 1)
                    for k in range(GR):
                        ins = v.scalar_tensor_tensor(out=x1[par][:, g * GR + k, :], in0=ps_pv[g][:, k * D:(k + 1) * D],
                                                     scalar=rsum[:, g * GR + k:g * GR + k + 1], in1=xs[par][:, g * GR + k, :],
                                                     op0=ALU.mult, op1=ALU.add)
                    ins.then_inc(x1_done, 1)
                dve.wait_ge(x1_done, 2 * c + 2)
                left = [(1, k) for k in range(CH)] + ([(0, k) for k in range(CH)] if beyond else [])

                def fill():
                    if left:
                        w, k = left.pop(0)
                        if w == 0 and k % GR == 0:
                            dve.wait_ge(x_in[par][k // GR], 16 * (r + 2))
                        S.did(v.bn_stats(stat[:, w, k, :], (xs, x1)[w][par][:, k, :]))

                if prev:
                    for k in range(CH // 2):
                        fill()
                    gate(c - 1, fill)
                while left:
                    fill()
                S.wait(S.n)
                mean_and_var(slice(0 if beyond else 1, 2)).then_inc(moments, 1)

            start = [0, 0]

            def attention(r, first, last):
                if not first and not last:
                    S.base, S.n = start[0] + (r - 1) * PER_ROUND, 0
                if last:
                    S.base, S.n = start[0] + (ROUNDS - 2) * PER_ROUND, 0
                for par in range(2):
                    chunk(2 * r + par, par, r, not first, not first or par == 1, not last or par == 0, not last)
                if first:
                    start[0] = S.base + S.n
                elif not last:
                    assert S.n == PER_ROUND, S.n

            PER_ROUND = 102
            rounds(dve, ROUNDS, attention)
            places(0, NC - 2, odds_sum(NC - 2), rank_in_all(NC - 2))
            dve.wait_ge(guess, NC + 2)
            rstd(SECOND)
            norm_u(NC - 1, 1, ROUNDS - 1)
            gate(NC - 1, lambda: None)
            places(1, NC - 1, odds_sum(NC - 1), rank_in_all(NC - 1))

            dve.wait_ge(loaded, 16 * LOADS)
            dve.wait_ge(count_done, 1)
            v.tensor_tensor(tail_i[:], ps_gate[:, 0:E], region[:], ALU.add).then_inc(tails_ready, 1)
            S.wait(S.did(v.tensor_scalar(tiles_i[:], ps_h[0:E, 0:P], 1.0 / T, (T - 1) / (2.0 * T), ALU.mult, ALU.add)))
            v.tensor_copy(tiles_b[:], tiles_i[:]).then_inc(tiles_ready, 1)
            dve.wait_ge(cum_done, 1)
            S.wait(S.did(v.tensor_copy(cums[:], ps_h[:, 0:3 * E])))
            S.did(v.tensor_scalar(skip[:], cums[:, 2 * E:], -1.0, float(REGION // T), ALU.mult, ALU.add))
            S.wait(S.did(v.tensor_tensor(tab_cmp[:], bc(iota_t[:], [P, E]), cums[:, 0:E], ALU.is_ge)))
            S.did(v.tensor_tensor(tab_mul[:], tab_cmp[:], skip[:], ALU.mult))
            s = S.did(v.tensor_reduce(tab[:, 2:3], tab_cmp[:], X, ALU.add))
            S.wait(s - 1)
            S.did(v.tensor_reduce(tab[:, 3:4], tab_mul[:], X, ALU.add))
            S.wait(s)
            S.did(v.tensor_scalar(tab[:, 0:1], tab[:, 2:3], float(E - 1), None, ALU.min))
            S.wait(s + 1)
            S.wait(S.did(v.tensor_tensor(tab[:, 4:5], tab[:, 3:4], iota_t[:], ALU.add)))
            v.tensor_scalar(tab[:, 1:2], tab[:, 4:5], float(T), None, ALU.mult).then_inc(tab_ready, 1)
            dve.wait_ge(tab_done, 1)
            v.tensor_copy(tab_i[:], ps_h[0:2, 0:P]).then_inc(tables_ready, 1)
            dve.wait_ge(tables_ready, 1)

            def tile_weights(i, q):
                e = dve.value_load(tab_i[0:1, bass.ds(i, 1)], min_val=0, max_val=E - 1)
                wait(dve, y_added, i - YRING + 1)
                v.tensor_scalar(wts[q % YRING][:], w1_sb[:, bass.ds(e * WB, WB)], 1.0, None, ALU.mult).then_inc(wts_ready, 1)

            def tiles(r, first, last):
                for q in range(LAST if last else RING):
                    i = RING * r + q
                    if not (last and q >= LAST - (YRING - 1)):
                        tile_weights(i + YRING - 1, q + YRING - 1)
                    wait(dve, y_sent[(q - YRING) % RING], 32 * (r + (q >= YRING)))
                    dve.wait_ge(y_done, i + 1)
                    v.tensor_tensor(y_sb[q % YRING][:], ps_y[q % 2][:, 0:T].rearrange("p (k d) -> p k d", k=2),
                                    bc(wts[q % YRING][:, F + FH:].unsqueeze(1), [P, 2, D]), ALU.add).then_inc(y_biased, 1)
                    dve.wait_ge(y_biased, i + 1)
                    v.tensor_tensor(y_sb[q % YRING][:], y_sb[q % YRING][:], bc(rows[q][:, :, D + 1:D + 2], [P, 2, D]),
                                    ALU.mult).then_inc(y_added, 1)

            for q in range(YRING - 1):
                tile_weights(q, q)
            for par in range(2):
                dve.wait_ge(x1_kept[par], 16 * ROUNDS)
            v.tensor_tensor(x1_all[:], x1_all[:], bc(beta_sb[:].unsqueeze(1), [P, NC * CH, D]), ALU.add).then_inc(beta_added, 1)
            rounds(dve, TROUNDS, tiles)

            S.base, S.n = S.base + S.n, 0

            def add_first(c, par, r):
                dve.wait_ge(c_in[par], 32 * (r + 1))
                wait(dve, c_normed, c - 1)
                for g in range(2):
                    half = slice(g * GR, (g + 1) * GR)
                    v.tensor_tensor(u[par][1][:, half, 0:D], u[par][0][:, half, 0:D], yt[par][:, half, 0:D],
                                    ALU.add).then_inc(c_first, 1)

            def combine(r, first, last):
                if not first and not last:
                    S.base, S.n = start[0] + (r - 1) * C_ROUND, 0
                if last:
                    S.base, S.n = start[0] + (ROUNDS - 2) * C_ROUND, 0
                for par in range(2):
                    c = 2 * r + par
                    acc = u[par][1][:, :, 0:D]
                    for g in range(2):
                        dve.wait_ge(c_first, 2 * c + g + 1)
                        half = slice(g * GR, (g + 1) * GR)
                        v.tensor_tensor(acc[:, half, :], acc[:, half, :], yt[par][:, half, D:2 * D], ALU.add).then_inc(c_summed, 1)
                    for k in range(CH):
                        if k % GR == 0:
                            dve.wait_ge(c_summed, 2 * c + k // GR + 1)
                        S.did(v.bn_stats(stat[:, 1, k, :], acc[:, k, :]))
                    S.wait(S.n)
                    mean_and_var(SECOND).then_inc(c_moments, 1)
                    if not last or par == 0:
                        add_first(c + 1, 1 - par, r + par)
                    dve.wait_ge(c_guess, c + 1)
                    rstd(SECOND)
                    offset(SECOND).then_inc(c_scale, 1)
                if first:
                    start[0] = S.base + S.n
                elif not last:
                    assert S.n == C_ROUND, S.n

            C_ROUND = 2 * (CH + 6 + 4)
            add_first(0, 0, 0)
            rounds(dve, ROUNDS, combine)
            for g in range(2):
                half = slice(g * GR, (g + 1) * GR)
                dve.wait_ge(c_normed, NC - 1 + g + 1)
                S.wait(S.did(v.tensor_tensor(xn[1][:, half], xn[1][:, half], bc(gamma_sb[:].unsqueeze(1), [P, GR, D]), ALU.mult)))
                v.tensor_tensor(xn[1][:, half], xn[1][:, half],
                                x1_all[:, (NC - 1) * CH + g * GR:(NC - 1) * CH + (g + 1) * GR], ALU.add).then_inc(last_ready, 1)

        @block.scalar
        def _(act):
            s = nc.scalar

            def guess_of(w, n, done):
                s.activation(nrm[:, 8, w], nrm[:, 6, w], ACT.Ln).then_inc(ln_done, 1)
                act.wait_ge(ln_done, n)
                s.activation(nrm[:, 7, w], nrm[:, 8, w], ACT.Exp, scale=-0.5).then_inc(done, 1)

            def guess_next(n, w):
                act.wait_ge(moments, n)
                guess_of(w, n, guess)

            def norm_rows(dst, src, w, ks):
                for k in ks:
                    ins = s.activation(dst[:, k, :], src[:, k, 0:D], ACT.Identity, bias=nrm[:, 10, w, k:k + 1],
                                       scale=nrm[:, 9, w, k:k + 1])
                return ins

            def norm_rest(c, par):
                act.wait_ge(scale1, c + 1)
                norm_rows(xn[par], xs[par], 0, range(SHARE, GR)).then_inc(xn_ready[0], 1)
                norm_rows(xn[par], xs[par], 0, range(GR, CH)).then_inc(xn_ready[1], 1)

            def turned(c):
                for g in range(2):
                    act.wait_ge(xT_done, 2 * c + g + 1)
                    s.activation(xT[g][:], ps_xT[g][:], ACT.Copy).then_inc(xT_ready, 1)

            def scored(c):
                for g in range(2):
                    act.wait_ge(z_done, 2 * c + g + 1)
                    s.activation(z02[g][:], ps_z[g][:], ACT.Copy, scale=SLOPE).then_inc(y_ready, 1)

            def projected(c, par):
                for g in range(2):
                    act.wait_ge(h_done, 2 * c + g + 1)
                    s.activation(h_sb[par][g][:], ps_hg[g][:], ACT.Copy).then_inc(h_ready, 1)

            def u_turned(c, g):
                act.wait_ge(uT_done, 2 * c + g + 1)
                s.activation(uT[g][:], ps_u[:], ACT.Copy).then_inc(uT_ready, 1)

            def u_copied(c, par):
                act.wait_ge(u_ready, 2 * c + 2)
                s.activation(u[par][1][:, :, 0:D], u[par][0][:, :, 0:D], ACT.Copy).then_inc(u2_ready, 1)

            def odds(c):
                act.wait_ge(gap_ready, c + 1)
                s.activation(top[:, 5, :], top[:, 4, :], ACT.Exp).then_inc(odds_ready, 1)

            def chunk(c, par, prev, ahead, beyond):
                for g in range(2):
                    act.wait_ge(max_ready, 2 * c + g + 1)
                    for k in range(GR):
                        ins = s.activation(prob[g][:, k, :], score[g][:, k, :], ACT.Exp, bias=negmax[g][:, k:k + 1],
                                           accum_out=sums[:, g * GR + k:g * GR + k + 1])
                    ins.then_inc(exp_ready, 1)
                for g in range(2):
                    act.wait_ge(pT_done, 2 * c + g + 1)
                    s.activation(pT[g][:], ps_pT[g][:], ACT.Copy).then_inc(pT_ready, 1)
                if ahead:
                    norm_rest(c + 1, 1 - par)
                if prev:
                    for g in range(2):
                        u_turned(c - 1, g)
                if ahead:
                    turned(c + 1)
                if prev:
                    u_copied(c - 1, 1 - par)
                if ahead:
                    scored(c + 1)
                if prev:
                    odds(c - 1)
                guess_next(c + 3, slice(0 if beyond else 1, 2))
                if ahead:
                    projected(c + 1, 1 - par)

            s.preload_act_table_set("natural_log_exp_and_others")
            guess_next(1, FIRST)
            norm_rest(0, 0)
            turned(0)
            scored(0)
            guess_next(2, FIRST)
            projected(0, 0)

            def attention(r, first, last):
                for par in range(2):
                    chunk(2 * r + par, par, not first or par == 1, not last or par == 0, not last)

            rounds(act, ROUNDS, attention)
            for g in range(2):
                u_turned(NC - 1, g)
            u_copied(NC - 1, 1)
            odds(NC - 1)

            act.wait_ge(tails_ready, 1)
            empty_tails(act, 1)

            def evacuate(i, q):
                act.wait_ge(rowsT_done, i + 1)
                s.activation(rowsT[q % 2][:], ps_rT[q % 2][:, 0:T], ACT.Copy).then_inc(rowsT_ready, 1)

            def hidden(i, q):
                if not (isinstance(i, int) and i < 2):
                    act.wait_ge(y_done, i - 1)
                for j in range(FH):
                    act.wait_ge(hid_done, FH * i + j + 1)
                    s.activation(hid[q % 2][j][:], ps_hid[j][:, 0:T], ACT.Relu,
                                 bias=wts[q % YRING][:, F + j:F + j + 1]).then_inc(hid_ready, 1)

            def tiles(r, first, last):
                for q in range(LAST if last else RING):
                    i = RING * r + q
                    if not (last and q == LAST - 1):
                        evacuate(i + 1, q + 1)
                        hidden(i + 1, q + 1)

            evacuate(0, 0)
            hidden(0, 0)
            rounds(act, TROUNDS, tiles)

            def combine(r, first, last):
                for par in range(2):
                    c = 2 * r + par
                    act.wait_ge(c_moments, c + 1)
                    guess_of(SECOND, NC + 2 + c + 1, c_guess)
                    wait(act, out_done[par], 16 * r)
                    act.wait_ge(c_scale, c + 1)
                    if last and par == 1:
                        norm_rows(xn[par], u[par][1], 1, range(GR)).then_inc(c_normed, 1)
                        norm_rows(xn[par], u[par][1], 1, range(GR, CH)).then_inc(c_normed, 1)
                    else:
                        norm_rows(xn[par], u[par][1], 1, range(CH)).then_inc(c_normed, 1)

            rounds(act, ROUNDS, combine)

        @block.tensor
        def _(pe):
            t = nc.tensor

            def mm(out_, lhsT, rhs, start=True, stop=True):
                return t.matmul(out_, lhsT, rhs, start=start, stop=stop)

            pe.wait_ge(ident_set, 1)
            pe.wait_ge(small_in, 16 * SMALL)
            t.transpose(ps_gate[:, 0:D], W_sb[:], ident[:]).then_inc(prep_done, 1)
            pe.wait_ge(prep_copied, 1)
            mm(ps_gate[:, 0:2], W_sb[:], a_sb[:]).then_inc(prep_done, 1)

            def turn_x(c, par, g):
                pe.wait_ge(xn_ready[g], (2 - g) * (c + 1))
                if g == 0:
                    wait(pe, h_ready, 2 * c - 1)
                else:
                    wait(pe, x1_done, 2 * c - 1)
                for k in range(GR):
                    ins = t.transpose(ps_xT[g][:, k * N:(k + 1) * N], xn[par][:, g * GR + k, :], ident[:])
                ins.then_inc(xT_done, 1)

            def scores(c, g):
                n = 2 * c + g
                pe.wait_ge(xT_ready, n + 1)
                pe.wait_ge(mask_ready, n + 1)
                mm(ps_z[g][:], v_rep[:, 1, :], xT[g][:], True, False)
                for k in range(GR):
                    mm(ps_z[g][:, k * N:(k + 1) * N], xT[g][:, k * N:(k + 1) * N], v_rep[:, 0, :], False, False)
                mm(ps_z[g][:], ident_b[:], mask[g][:], False, True).then_inc(z_done, 1)

            def project(c, g):
                if g == 1:
                    wait(pe, pT_ready, 2 * c - 1)
                for k in range(GR):
                    ins = mm(ps_hg[g][:, k * D:(k + 1) * D], xT[g][:, k * N:(k + 1) * N], WT[:])
                ins.then_inc(h_done, 1)

            def turn_probs(c, g):
                pe.wait_ge(exp_ready, 2 * c + g + 1)
                if g == 0:
                    pe.wait_ge(h_ready, 2 * c + 2)
                else:
                    wait(pe, uT_ready, 2 * c - 2)
                for k in range(GR):
                    ins = t.transpose(ps_pT[g][:, k * N:(k + 1) * N], prob[g][:, k, :], ident[:])
                ins.then_inc(pT_done, 1)

            def aggregate(c, par, g):
                n = 2 * c + g
                pe.wait_ge(pT_ready, n + 1)
                wait(pe, x1_done, n - 1)
                for k in range(GR):
                    ins = mm(ps_pv[g][:, k * D:(k + 1) * D], pT[g][:, k * N:(k + 1) * N], h_sb[par][g][:, k * D:(k + 1) * D])
                ins.then_inc(pv_done, 1)

            def turn_u(c, par, g, probs):
                n = 2 * c + g
                pe.wait_ge(u_ready, n + 1)
                if g == 0:
                    pe.wait_ge(pT_ready, probs)
                wait(pe, uT_ready, n)
                for k in range(GR):
                    ins = t.transpose(ps_u[:, k * N:(k + 1) * N], u[par][0][:, g * GR + k, 0:D], ident[:])
                ins.then_inc(uT_done, 1)

            def logits(c):
                wait(pe, pos_ready, c)
                for g in range(2):
                    pe.wait_ge(uT_ready, 2 * c + g + 1)
                    for k in range(GR):
                        at = (g * GR + k) * E
                        ins = mm(ps_gate[:, at:at + E], uT[g][:, k * N:(k + 1) * N], gw[:])
                ins.then_inc(gate_done, 1)

            def ranks(c):
                pe.wait_ge(both_ready, c + 1)
                flat = both_b[:].rearrange("p k e -> p (k e)")
                w = CH * E
                mm(ps_gate[:, w:2 * w], before_b[:], flat, True, False)
                for k in range(1, CH):
                    mm(ps_gate[:, w + k * E:2 * w], ones_b[:], flat[:, 0:(CH - k) * E], False, False)
                wait(pe, seen_ready, c)
                mm(ps_gate[:, w:2 * w], ones_b[:], seen_b[:].unsqueeze(1).to_broadcast([P, CH, E]),
                   False, True).then_inc(rank_done, 1)

            def attention(r, first, last):
                for par in range(2):
                    c = 2 * r + par
                    prev = not first or par == 1
                    ahead = not last or par == 0
                    for g in range(2):
                        turn_probs(c, g)
                    for g in range(2):
                        aggregate(c, par, g)
                        if prev:
                            turn_u(c - 1, 1 - par, g, 2 * c + 2)
                    if prev:
                        logits(c - 1)
                    if ahead:
                        for g in range(2):
                            turn_x(c + 1, 1 - par, g)
                        for g in range(2):
                            scores(c + 1, g)
                    if prev:
                        ranks(c - 1)
                    if ahead:
                        for g in range(2):
                            project(c + 1, g)

            for g in range(2):
                turn_x(0, 0, g)
            pe.wait_ge(prep_copied, 2)
            pe.wait_ge(consts, 1)
            pe.wait_ge(pool_done, POOL_CONSTS)
            for g in range(2):
                scores(0, g)
            for g in range(2):
                project(0, g)
            rounds(pe, ROUNDS, attention)
            for g in range(2):
                turn_u(NC - 1, 1, g, 2 * NC)
            logits(NC - 1)
            ranks(NC - 1)

            pe.wait_ge(seen_ready, NC)
            mm(ps_gate[:, 0:E], ones_b[:], seen_b[:])
            mm(ps_h[0:E, 0:P], seen_b[:], ones_b[:]).then_inc(count_done, 1)
            pe.wait_ge(tiles_ready, 1)
            mm(ps_h[:, 0:3 * E], tiles_b[:], cum48[:]).then_inc(cum_done, 1)
            pe.wait_ge(tab_ready, 1)
            t.transpose(ps_h[0:2, 0:P], tab[:, 0:2], ident[:]).then_inc(tab_done, 1)
            pe.wait_ge(tables_ready, 1)

            def turn_rows(i, q, r):
                pe.wait_ge(rows_in[q % RING], 16 * (r + 1))
                wait(pe, rowsT_ready, i - 1)
                for k in range(2):
                    ins = t.transpose(ps_rT[q % 2][:, k * P:(k + 1) * P], rows[q % RING][:, k, 0:D], ident[:])
                ins.then_inc(rowsT_done, 1)

            def hidden(i, q):
                pe.wait_ge(rowsT_ready, i + 1)
                pe.wait_ge(wts_ready, i + 1)
                wait(pe, hid_ready, FH * i)
                for j in range(FH):
                    mm(ps_hid[j][:, 0:T], wts[q % YRING][:, j * P:(j + 1) * P], rowsT[q % 2][:]).then_inc(hid_done, 1)

            def results(i, q, e):
                wait(pe, y_biased, i - 1)
                for j in range(FH):
                    pe.wait_ge(hid_ready, FH * i + j + 1)
                    for k in range(2):
                        ins = mm(ps_y[q % 2][:, k * D:(k + 1) * D], hid[q % 2][j][:, k * P:(k + 1) * P],
                                 w2_sb[:, bass.ds(e * (FH * D) + j * D, D)], j + k == 0, j + k == FH)
                ins.then_inc(y_done, 1)

            def expert_of(i):
                return pe.value_load(tab_i[0:1, bass.ds(i, 1)], min_val=0, max_val=E - 1)

            def tiles(r, first, last):
                for q in range(LAST if last else RING):
                    i = RING * r + q
                    if first and q == 0:
                        results(i, q, expert_of(i))
                    if not (last and q == LAST - 1):
                        hidden(i + 1, q + 1)
                    if not (first and q == 0):
                        e = expert_of(i)
                    if not (last and q >= LAST - 2):
                        turn_rows(i + 2, q + 2, r + (q + 2) // RING)
                    if not (first and q == 0):
                        results(i, q, e)

            turn_rows(0, 0, 0)
            hidden(0, 0)
            turn_rows(1, 1, 0)
            rounds(pe, TROUNDS, tiles)

        @block.gpsimd
        def _(pool):
            p = nc.gpsimd
            S = Steps(pool, pool_done)
            S.wait(S.did(p.memset(ident[:], 1.0)))
            p.affine_select(ident[:], ident[:], pattern=[[-1, P]], compare_op=ALU.is_equal, fill=0.0, base=0,
                            channel_multiplier=1).then_inc(ident_set, 1)
            S.did(p.memset(cum48[:], 1.0))
            for par in range(2):
                for j in range(K):
                    p.memset(u[par][j][:, :, D:RW], 0.0)
            p.memset(empty[:], 0.0)
            S.wait(S.did(p.memset(before_b[:], 1.0)))
            S.did(p.affine_select(before_b[:], before_b[:], pattern=[[1, P]], compare_op=ALU.is_gt, fill=0.0, base=0,
                                  channel_multiplier=-1))
            for n, op in enumerate((ALU.is_ge, ALU.is_gt, ALU.is_equal)):
                S.did(p.affine_select(cum48[:, n * E:(n + 1) * E], cum48[:, n * E:(n + 1) * E], pattern=[[1, E]],
                                      compare_op=op, fill=0.0, base=0, channel_multiplier=-1))
            S.did(p.iota(iota_e[:], pattern=[[1, E]], base=0, channel_multiplier=0, allow_small_or_imprecise_dtypes=True))
            S.did(p.iota(region[:], pattern=[[REGION, E]], base=0, channel_multiplier=0, allow_small_or_imprecise_dtypes=True))
            S.did(p.iota(iota_t[:], pattern=[[0, 1]], base=0, channel_multiplier=1, allow_small_or_imprecise_dtypes=True))
            for par in range(2):
                for j in range(K):
                    ins = p.iota(u[par][j][:, :, D].bitcast(I32), pattern=[[N * K, CH]],
                                 base=par * CH * N * K + j - 2 * CH * N * K, channel_multiplier=K)
            S.did(ins)
            S.did(p.iota(empty[:, :, D].bitcast(I32), pattern=[[0, FILL]], base=NOWHERE, channel_multiplier=0))
            S.did(p.memset(empty[:, :, D + 1:], 0.0))

            def send(r, first, last):
                for par in range(2):
                    pool.wait_ge(pos_ready, 2 * r + par + 1)
                    pool.wait_ge(u2_ready, 2 * r + par + 1)
                    pool.sem_inc(pool_turns, 1)
                    for j in range(K):
                        for k in range(CH):
                            p.indirect_dma_start(xs_buf, bass.IndirectOffsetOnAxis(ap=pos[par][:, j * CH + k:j * CH + k + 1], axis=0),
                                                 u[par][j][:, k, :], None).then_inc(sent[par], 16)

            rounds(pool, ROUNDS, send)

            def send_results(r, first, last):
                for q in range(LAST if last else RING):
                    alone = first and q < 2 or last and q >= LAST - 2
                    if alone or q % 2 == 0:
                        pool.wait_ge(y_added, RING * r + q + (1 if alone else 2))
                        pool.sem_inc(pool_turns, 1)
                    for k in range(2):
                        p.indirect_dma_start(y_buf, bass.IndirectOffsetOnAxis(ap=rows[q][:, k, D:D + 1].bitcast(U32), axis=0),
                                             y_sb[q % YRING][:, k, :], None, bounds_check=TOK * K - 1,
                                             oob_is_err=False).then_inc(y_sent[q], 16)

            rounds(pool, TROUNDS, send_results)

            pool.wait_ge(beta_added, 1)

            def combine(r, first, last):
                for par in range(2):
                    c = 2 * r + par
                    if last and par == 1:
                        break
                    pool.wait_ge(c_normed, c + 1)
                    p.tensor_tensor(xn[par][:], xn[par][:], gamma_sb[:].unsqueeze(1).to_broadcast([P, CH, D]),
                                    ALU.mult).then_inc(c_scaled, 1)
                    pool.wait_ge(c_scaled, c + 1)
                    pool.sem_inc(pool_turns, 1)
                    p.tensor_tensor(xn[par][:], xn[par][:], x1_all[:, bass.ds(c * CH, CH), :], ALU.add).then_inc(out_ready, 1)

            rounds(pool, ROUNDS, combine)


_INS = ["x", "adj", "L0_gnn_W", "L0_gnn_a", "L0_ffn_gate_w", "L0_ffn_gate_b", "L0_ffn_w1", "L0_ffn_b1", "L0_ffn_w2",
        "L0_ffn_b2", "L0_ffn_gamma", "L0_ffn_beta"]


def kernel(**inputs):
    import numpy as _np
    import concourse.bacc as _bacc
    from concourse import mybir as _mybir
    from concourse.bass_utils import run_bass_kernel_spmd as _run

    nc = _bacc.Bacc("TRN2", target_bir_lowering=False, num_devices=1)
    arrays, args = {}, []
    for name in _INS:
        arr = _np.ascontiguousarray(inputs[name])
        arrays[f"in_{name}"] = arr
        args.append(nc.dram_tensor(f"in_{name}", arr.shape, _mybir.dt.from_np(arr.dtype), kind="ExternalInput").ap())
    out = nc.dram_tensor("out_0", (G, N, D), _mybir.dt.float32, kind="ExternalOutput").ap()
    build(nc, *args, out)
    r = _run(nc, [arrays], core_ids=[0])
    return r.results[0]["out_0"]
```
